# Optimizing a Trainium2 kernel written in Bass

```python
import numpy as np
import jax
import jax.numpy as jnp

def _softmax(x, axis=-1):
    return jax.nn.softmax(x, axis=axis)

def _gelu(x):
    return jax.nn.gelu(x, approximate=True)

def _silu(x):
    return jax.nn.silu(x)

def _sigmoid(x):
    return jax.nn.sigmoid(x)

def _layernorm(x, axis=-1, eps=1e-05):
    m = jnp.mean(x, axis=axis, keepdims=True)
    v = jnp.var(x, axis=axis, keepdims=True)
    return (x - m) / jnp.sqrt(v + eps)

def _scatter_add(tgt, idx, src, axis=0):
    return tgt.at[idx].add(src)

def _segment_sum(src, seg, n):
    return jax.ops.segment_sum(src, seg, n)
kernel_name = 'mk_xattn_ffn_d1_seqx_r2_d099cc'

def setup_inputs(seed: int=0):
    np.random.seed(seed)
    _w = jnp.asarray

    def _rec_inputs():
        import jax
        import jax.numpy as jnp
        _rk = jax.random.key(seed)
        x = -0.000125 + 0.9999 * jax.random.normal(jax.random.fold_in(_rk, 1), (32, 512, 512), jnp.float32)
        _lenS = 512 - jax.random.randint(jax.random.fold_in(_rk, 7), (32,), 0, max(1, 512 // 4) + 1, jnp.int32)
        _lenS2 = 512 - jax.random.randint(jax.random.fold_in(_rk, 8), (32,), 0, max(1, 512 // 4) + 1, jnp.int32)
        _ctx_1024P = jax.random.normal(jax.random.fold_in(_rk, 11), (32, 16, 512), jnp.float32)
        _ctx_1024c = jax.random.dirichlet(jax.random.fold_in(_rk, 511), 0.3 * jnp.ones((16,), jnp.float32), (32, 512))
        _ctx_1024t = jnp.einsum('bsk,bkd->bsd', _ctx_1024c, _ctx_1024P)
        _ctx_1024t = _ctx_1024t * jax.lax.rsqrt(jnp.mean(jnp.square(_ctx_1024t)) + 1e-12) * 0.953939
        ctx_1024 = -1.52775e-05 + 0.999936 * (_ctx_1024t + 0.3 * jax.random.normal(jax.random.fold_in(_rk, 611), (32, 512, 512), jnp.float32))
        return (x, ctx_1024)
    x, ctx_1024 = _rec_inputs()

    def _L0_xattn_setup():
        import jax, jax.numpy as jnp
        import numpy as np
        DECAY = 0.9
        key = jax.random.key(seed)
        k1, k2, k3 = jax.random.split(key, 3)
        B, S, D = (8, 2048, 512)
        q = jax.random.normal(k1, (B, S, D), dtype=jnp.float32)
        k = jax.random.normal(k2, (B, S, D), dtype=jnp.float32)
        v = jax.random.normal(k3, (B, S, D), dtype=jnp.float32)
        return {'q': q, 'k': k, 'v': v}
    _L0_xattn_all = _L0_xattn_setup()
    _L0_xattn_in = {k: v for k, v in _L0_xattn_all.items() if k in ()}
    del _L0_xattn_all

    def _L0_ffn_setup():
        import jax, jax.numpy as jnp
        import numpy as np
        EPS = 1e-08

        def _ste(x, q):
            return x + jax.lax.stop_gradient(q - x)

        def quant_act_uint8(x):
            s = jax.lax.stop_gradient(jnp.maximum(jnp.max(x), EPS)) / 255.0
            q = jnp.clip(jnp.round(x / s), 0.0, 255.0) * s
            return (_ste(x, q), s)

        def quant_weight_int8_perchannel(w):
            s = jax.lax.stop_gradient(jnp.maximum(jnp.max(jnp.abs(w), axis=1, keepdims=True), EPS)) / 127.0
            q = jnp.clip(jnp.round(w / s), -128.0, 127.0) * s
            return (_ste(w, q), s[:, 0])

        def quant_bias_int32(b, s_in, s_w):
            s = jax.lax.stop_gradient(s_in * s_w)
            q = jnp.round(b / s) * s
            return _ste(b, q)

        def quant_linear(x, w, b):
            xq, s_in = quant_act_uint8(x)
            wq, s_w = quant_weight_int8_perchannel(w)
            bq = quant_bias_int32(b, s_in, s_w)
            return jnp.einsum('btd,fd->btf', xq, wq) + bq
        key = jax.random.key(seed)
        k1, k2, k3, k4, k5 = jax.random.split(key, 5)
        B, S, D, F = (4, 1024, 512, 2048)
        return {'x': jax.random.normal(k1, (B, S, D), dtype=jnp.float32), 'w1': jax.random.normal(k2, (F, D), dtype=jnp.float32) * (1.0 / np.sqrt(D)), 'b1': jax.random.normal(k3, (F,), dtype=jnp.float32) * 0.01, 'w2': jax.random.normal(k4, (D, F), dtype=jnp.float32) * (1.0 / np.sqrt(F)), 'b2': jax.random.normal(k5, (D,), dtype=jnp.float32) * 0.01}
    _L0_ffn_all = _L0_ffn_setup()
    _L0_ffn_in = {k: v for k, v in _L0_ffn_all.items() if k in ('w1', 'b1', 'w2', 'b2')}
    del _L0_ffn_all
    return {'x': x, 'ctx_1024': ctx_1024, 'L0_ffn_w1': _L0_ffn_in['w1'], 'L0_ffn_b1': _L0_ffn_in['b1'], 'L0_ffn_w2': _L0_ffn_in['w2'], 'L0_ffn_b2': _L0_ffn_in['b2']}

def reference(x, ctx_1024, L0_ffn_w1, L0_ffn_b1, L0_ffn_w2, L0_ffn_b2):
    import jax
    import jax.numpy as jnp

    def _L0_xattn_ref(q, k, v):
        import jax, jax.numpy as jnp
        import numpy as np
        DECAY = 0.9
        kv = jnp.swapaxes(k * v, 0, 1)

        def step(r, kv_t):
            r = DECAY * r + kv_t
            return (r, r)
        r0 = jnp.zeros(q.shape[:1] + q.shape[2:], dtype=q.dtype)
        _, rs = jax.lax.scan(step, r0, kv)
        return q * jnp.swapaxes(rs, 0, 1)

    def _L0_ffn_ref(x, w1, b1, w2, b2):
        import jax, jax.numpy as jnp
        import numpy as np
        EPS = 1e-08

        def _ste(x, q):
            return x + jax.lax.stop_gradient(q - x)

        def quant_act_uint8(x):
            s = jax.lax.stop_gradient(jnp.maximum(jnp.max(x), EPS)) / 255.0
            q = jnp.clip(jnp.round(x / s), 0.0, 255.0) * s
            return (_ste(x, q), s)

        def quant_weight_int8_perchannel(w):
            s = jax.lax.stop_gradient(jnp.maximum(jnp.max(jnp.abs(w), axis=1, keepdims=True), EPS)) / 127.0
            q = jnp.clip(jnp.round(w / s), -128.0, 127.0) * s
            return (_ste(w, q), s[:, 0])

        def quant_bias_int32(b, s_in, s_w):
            s = jax.lax.stop_gradient(s_in * s_w)
            q = jnp.round(b / s) * s
            return _ste(b, q)

        def quant_linear(x, w, b):
            xq, s_in = quant_act_uint8(x)
            wq, s_w = quant_weight_int8_perchannel(w)
            bq = quant_bias_int32(b, s_in, s_w)
            return jnp.einsum('btd,fd->btf', xq, wq) + bq
        h = jax.nn.relu(quant_linear(x, w1, b1))
        return quant_linear(h, w2, b2)
    x = x + _L0_xattn_ref(_layernorm(x, axis=-1), ctx_1024, ctx_1024)
    x = x + _L0_ffn_ref(_layernorm(x, axis=-1), L0_ffn_w1, L0_ffn_b1, L0_ffn_w2, L0_ffn_b2)
    return x

_drawn_inputs = setup_inputs


def setup_inputs(seed=0):
    import zlib

    import numpy as np

    out = dict(_drawn_inputs(seed))
    spreads = {}
    factors = {'L0_ffn_b1': 64.0, 'L0_ffn_b2': 64.0}
    for name, (base, spread) in spreads.items():
        noise = np.random.default_rng([zlib.crc32(name.encode()), seed]).standard_normal(out[name].shape)
        drawn = base * np.exp(spread * noise) if base else spread * noise
        out[name] = jnp.asarray(drawn.astype(out[name].dtype))
    for name, factor in factors.items():
        out[name] = (out[name] * factor).astype(out[name].dtype)
    return out
```

```python
from contextlib import ExitStack

import concourse.bass as bass
from concourse import mybir

ALU = mybir.AluOpType
ACT = mybir.ActivationFunctionType
AX = mybir.AxisListType
F32 = mybir.dt.float32
BF16 = mybir.dt.bfloat16

P = 128
BANK = 512
DECAY = 0.9
LN_EPS = 1e-5
Q_EPS = 1e-8
ROUND_POS = 2.0 ** 23
ROUND_ANY = 1.5 * 2.0 ** 23
XS = 4
HQ = 8
OT = 2
HV = 4


def wait_count(eng, sem, count):
    if isinstance(count, int) and count <= 0:
        return
    eng.wait_ge(sem, count)


def build(nc, x, ctx_in, w1, b1, w2, b2, out):
    NB, S, D = x.shape
    F = w1.shape[0]
    NI = S // P
    KD = D // P
    NF = F // P
    NU = NB * NI
    ROW = NI * D
    assert D == BANK and S == BANK and NI == KD == 4 and NF % HQ == 0 and NB % XS == 0

    x_rows = x.rearrange("b (i p) d -> b p i d", p=P)
    ctx_rows = ctx_in.rearrange("b (i p) d -> b p i d", p=P)
    out_rows = out.rearrange("b (i p) d -> b p i d", p=P)
    w1_rows = w1.rearrange("(c p) d -> p c d", p=P)
    w2_rows = w2.rearrange("(k p) f -> p k f", p=P)
    b1_rows = b1.rearrange("(c p) -> c p", p=P)
    b2_rows = b2.rearrange("(k p) -> k p", p=P)
    x2_dram = nc.dram_tensor("x2_scratch", [NB, P, ROW], F32, kind="Internal").ap()

    with ExitStack() as es:
        def sb(name, shape, dt=F32):
            return es.enter_context(nc.sbuf_tensor(name, shape, dt))

        def sem(name):
            return es.enter_context(nc.semaphore(name))

        xq = sb("xq", [P, NB * KD * S], BF16)
        arena = xq[:, :].bitcast(F32)
        o = NF * D + NF * D // 2
        rs = [arena[:, o + n * ROW:o + (n + 1) * ROW].rearrange("p (i d) -> p i d", i=NI) for n in range(2)]
        o += 2 * ROW
        ct = [arena[:, o + n * ROW:o + (n + 1) * ROW].rearrange("p (i d) -> p i d", i=NI) for n in range(XS)]
        o += XS * ROW
        xt = [arena[:, o + n * ROW:o + (n + 1) * ROW].rearrange("p (i d) -> p i d", i=NI) for n in range(XS)]
        assert o + XS * ROW == NB * KD * S // 2

        w1T = sb("w1T", [P, KD, F], BF16)
        w2T = sb("w2T", [P, NF, D], BF16)
        ident = sb("ident", [P, P])
        ident_b = sb("ident_b", [P, P], BF16)
        ones = sb("ones", [P, P])
        diag = sb("diag", [P, P])
        st1 = sb("st1", [P, XS, NI, 6])
        st2 = sb("st2", [P, XS, NI, 6])
        rowmax = sb("rowmax", [P, XS, NI])
        pw = sb("pw", [P, 2, 10, NI])
        half = sb("half", [P, NI])
        neg_half = sb("neg_half", [P, NI])
        per_row = sb("per_row", [P, NI])
        eps = sb("eps", [P, NI])
        mean1 = sb("mean1", [P, XS, NI])
        rstd1 = sb("rstd1", [P, XS, NI])
        mean2 = sb("mean2", [P, NU])
        rstd2 = sb("rstd2", [P, NU])
        zrow = sb("zrow", [P, NU])
        qa = zrow
        qb = sb("qb", [P, NU])
        round_any = sb("round_any", [P, 1])
        wmax = [sb("wmax1", [P, NF]), sb("wmax2", [P, KD])]
        sw = [sb("sw1", [P, NF]), sb("sw2", [P, KD])]
        isw = [sb("isw1", [P, NF]), sb("isw2", [P, KD])]
        brow = sb("brow", [NF, P])
        brow2 = sb("brow2", [KD, P])
        b1c = sb("b1c", [P, NF])
        b2c = sb("b2c", [P, KD])
        rb = sb("rb", [P, 10, NF])
        s1 = sb("s1", [P, 1])
        is1 = sb("is1", [P, 1])
        s2 = sb("s2", [P, 1])
        is2 = sb("is2", [P, 1])
        cmax = sb("cmax", [P, 6])
        cs1 = sb("cs1", [P, NF])
        bq1 = sb("bq1", [P, NF])
        hm = sb("hm", [P, 3, NF])
        hs = sb("hs", [P, NF])
        hb = sb("hb", [P, NF])
        cs2 = sb("cs2", [P, KD])
        bq2 = sb("bq2", [P, KD])
        cs2_bc = sb("cs2_bc", [P, D])
        bq2_bc = sb("bq2_bc", [P, D])
        work = sb("work", [P, 4 * ROW + 2 * D])
        x2t = [work[:, n * ROW:(n + 1) * ROW].rearrange("p (i d) -> p i d", i=NI) for n in range(2)]
        qi = [work[:, (4 + n) * ROW // 2:(5 + n) * ROW // 2].bitcast(BF16).rearrange("p (i d) -> p i d", i=NI) for n in range(2)]
        hv = work[:, 2 * ROW:2 * ROW + HV * S].rearrange("p (n t) -> p n t", n=HV)
        hq = work[:, 3 * ROW:3 * ROW + HQ * S // 2].bitcast(BF16).rearrange("p (n t) -> p n t", n=HQ)
        ot = work[:, 4 * ROW:4 * ROW + OT * D].rearrange("p (i d) -> p i d", i=OT)
        decay_mat = work[:, 4 * ROW:4 * ROW + S]
        hmax = work[:, 4 * ROW + S:4 * ROW + S + NB * NF]
        diag_cs, diag_bq = ot[:, 0, :], ot[:, 1, :]
        w_stage = [arena[:, 0:NF * D], work[:, 0:4 * ROW]]
        w_int_rows = arena[:, NF * D:NF * D + NF * D // 2].bitcast(BF16)
        decays, impulse = xt[XS - 1][:, 0, :], xt[XS - 1][:, 1, :]

        ps = es.enter_context(nc.psum_tensor("ps", [P, 8, BANK], F32))

        consts_ready = sem("consts_ready")
        gp_step = sem("gp_step")
        ln1_step = sem("ln1_step")
        ln2_step = sem("ln2_step")
        dve_step = sem("dve_step")
        x_loaded = [sem(f"x_loaded{n}") for n in range(XS)]
        ctx_loaded = [sem(f"ctx_loaded{n}") for n in range(XS)]
        ctx_squared = sem("ctx_squared")
        scan_ready = sem("scan_ready")
        scan_scaled = sem("scan_scaled")
        stats1_in = sem("stats1_in")
        stats1_ready = sem("stats1_ready")
        prod_done = sem("prod_done")
        x2_done = sem("x2_done")
        stats2_in = sem("stats2_in")
        stats2_ready = sem("stats2_ready")
        x2_stored = [sem(f"x2_stored{n}") for n in range(XS)]
        w_loaded = [sem(f"w_loaded{n}") for n in range(2)]
        b_loaded = sem("b_loaded")
        w_scale = sem("w_scale")
        w_shifted = sem("w_shifted")
        w_int = sem("w_int")
        w_turned = sem("w_turned")
        w_kept = sem("w_kept")
        b_turned = sem("b_turned")
        b_kept = sem("b_kept")
        diag_ready = sem("diag_ready")
        spread_ready = sem("spread_ready")
        q_scales = sem("q_scales")
        x2_loaded = [sem(f"x2_loaded{n}") for n in range(2)]
        x_scaled = sem("x_scaled")
        x_int = sem("x_int")
        x_turned = sem("x_turned")
        xq_kept = sem("xq_kept")
        hid_ready = sem("hid_ready")
        hid_maxed = sem("hid_maxed")
        h_scales = sem("h_scales")
        h_ready = sem("h_ready")
        h_scaled = sem("h_scaled")
        h_int = sem("h_int")
        acc_ready = sem("acc_ready")
        acc_read = sem("acc_read")
        out_scales = sem("out_scales")
        hq_used = sem("hq_used")
        x2c_loaded = [sem(f"x2c_loaded{n}") for n in range(2)]
        bias_added = sem("bias_added")
        out_ready = sem("out_ready")
        out_stored = [sem(f"out_stored{n}") for n in range(2)]

        NG = NB // XS
        block = es.enter_context(nc.Block())

        def batches(eng, step):
            for j in range(XS):
                step(j, j, 0)
            with eng.Fori(1, NG) as g:
                for n in range(XS):
                    step(g * XS + n, n, g)

        def pairs(eng, step):
            for b in range(2):
                step(b, b, 0)
            with eng.Fori(1, NB // 2) as g:
                for n in range(2):
                    step(g * 2 + n, n, g)

        def singles(eng, step, straight=1):
            for b in range(straight):
                step(b)
            with eng.Fori(straight, NB) as b:
                step(b)

        def is_first(j, n=1):
            return isinstance(j, int) and j < n

        def tp_banks(n):
            return ps[:, 4 + 2 * n:6 + 2 * n, :].rearrange("p n e -> p (n e)").bitcast(BF16)

        @block.sync
        def _(sp):
            def store_x2(j, n):
                sp.wait_ge(x2_done, (j + 1) * NI)
                sp.dma_start(x2_dram[bass.ds(j, 1)].rearrange("b p m -> (b p) m"),
                             xt[n].rearrange("p i d -> p (i d)")).then_inc(x2_stored[n], 16)

            def phase_a(j, n, g):
                if isinstance(j, int) and j == XS - 1:
                    sp.wait_ge(dve_step, 1)
                if not is_first(j, XS):
                    sp.wait_ge(x2_stored[n], g * 16)
                sp.dma_start(xt[n], x_rows[bass.ds(j, 1)].rearrange("b p i d -> (b p) i d")).then_inc(x_loaded[n], 16)
                wait_count(sp, scan_ready, (j - XS + 1) * NI)
                sp.dma_start(ct[n], ctx_rows[bass.ds(j, 1)].rearrange("b p i d -> (b p) i d")).then_inc(ctx_loaded[n], 16)
                if is_first(j) :
                    sp.dma_start(brow[:, :], b1_rows).then_inc(b_loaded, 16)
                    sp.dma_start(brow2[:, :], b2_rows).then_inc(b_loaded, 16)
                    sp.dma_start(w_stage[0].rearrange("p (c d) -> p c d", c=NF), w1_rows).then_inc(w_loaded[0], 16)
                if isinstance(j, int) and j == 1:
                    sp.dma_start(w_stage[1].rearrange("p (k f) -> p k f", k=KD), w2_rows).then_inc(w_loaded[1], 16)
                if not is_first(j, 2):
                    store_x2(j - 2, (n - 2) % XS)

            batches(sp, phase_a)
            store_x2(NB - 2, XS - 2)
            store_x2(NB - 1, XS - 1)
            for n in range(XS):
                sp.wait_ge(x2_stored[n], 16 * NG)

            def load_x2(b, n, loaded):
                sp.dma_start(x2t[n].rearrange("p i d -> p (i d)"),
                             x2_dram[bass.ds(b, 1)].rearrange("b p m -> (b p) m")).then_inc(loaded[n], 16)

            def phase_b(b, n, g):
                if is_first(b):
                    sp.wait_ge(w_turned, 16)
                wait_count(sp, x_int, b - 1)
                load_x2(b, n, x2_loaded)

            pairs(sp, phase_b)
            sp.wait_ge(x_int, NB)

            def store_out(b, n):
                sp.wait_ge(out_ready, (b + 1) * NI)
                sp.dma_start(out_rows[bass.ds(b, 1)].rearrange("b p i d -> (b p) i d"), x2t[n]).then_inc(out_stored[n], 16)

            def phase_c(b, n, g):
                if not is_first(b, 2):
                    sp.wait_ge(out_stored[n], g * 16)
                load_x2(b, n, x2c_loaded)
                if not is_first(b):
                    store_out(b - 1, 1 - n)

            pairs(sp, phase_c)
            store_out(NB - 1, 1)
            for n in range(2):
                sp.wait_ge(out_stored[n], 16 * (NB // 2))

        @block.gpsimd
        def _(gp):
            gp.memset(round_any[:, :], ROUND_ANY)
            gp.memset(half[:, :], 0.5)
            gp.memset(per_row[:, :], 1.0 / D)
            gp.memset(eps[:, :], LN_EPS)
            gp.memset(ones[:, :], 1.0)
            gp.memset(decays, DECAY)
            gp.memset(neg_half[:, :], -0.5)
            gp.memset(impulse, 0.0)
            gp.memset(ident[:, :], 0.0)
            gp.memset(ident_b[:, :], 0.0).then_inc(gp_step, 1)
            gp.wait_ge(gp_step, 1)
            for m, w in ((impulse, S), (ident[:, :], P), (ident_b[:, :], P)):
                last = gp.affine_select(out=m, in_=m, compare_op=ALU.not_equal, fill=1.0, base=0,
                                        pattern=[[-1, w]], channel_multiplier=1)
            last.then_inc(consts_ready, 1)

            def row_stats(w, st, mean, done, base):
                me, mo, ve, vo = (st[:, :, k] for k in (1, 4, 2, 5))
                t = [pw[:, w, k, :] for k in range(8)]
                gp.tensor_tensor(t[0], me, mo, ALU.add)
                gp.tensor_tensor(t[1], ve, vo, ALU.add)
                gp.tensor_tensor(t[2], me, mo, ALU.subtract).then_inc(done, 1)
                gp.wait_ge(done, base + 1)
                gp.tensor_tensor(mean, t[0], half[:, :], ALU.mult)
                gp.tensor_tensor(t[3], t[1], per_row[:, :], ALU.mult)
                gp.tensor_tensor(t[4], t[2], half[:, :], ALU.mult).then_inc(done, 1)
                gp.wait_ge(done, base + 2)
                gp.tensor_tensor(t[5], t[3], eps[:, :], ALU.add)
                gp.tensor_tensor(t[6], t[4], t[4], ALU.mult).then_inc(done, 1)
                gp.wait_ge(done, base + 3)
                gp.tensor_tensor(t[7], t[5], t[6], ALU.add).then_inc(done, 1)
                return t[7]

            def second_stats(j, n):
                cols = bass.ds(j * NI, NI)
                wait_count(gp, stats2_ready, j)
                gp.wait_ge(stats2_in, j + 1)
                var = row_stats(1, st2[:, n], pw[:, 1, 8, :], ln2_step, j * 4)
                gp.wait_ge(ln2_step, j * 4 + 4)
                gp.tensor_tensor(pw[:, 1, 9, :], var, var, ALU.add)
                gp.tensor_tensor(rstd2[:, cols], var, neg_half[:, :], ALU.pow)
                gp.tensor_tensor(mean2[:, cols], pw[:, 1, 0, :], half[:, :], ALU.mult)
                gp.tensor_tensor(zrow[:, cols], rowmax[:, n, :], pw[:, 1, 8, :], ALU.subtract).then_inc(stats2_ready, 1)

            def phase_a(j, n, g):
                gp.wait_ge(stats1_in, j + 1)
                var = row_stats(0, st1[:, n], mean1[:, n, :], ln1_step, j * 4)
                gp.wait_ge(ln1_step, j * 4 + 4)
                gp.tensor_tensor(rstd1[:, n, :], var, neg_half[:, :], ALU.pow).then_inc(stats1_ready, 1)
                if not is_first(j):
                    second_stats(j - 1, (n - 1) % XS)
                if isinstance(j, int) and j in (1, 2):
                    gp.wait_ge(w_shifted, j)
                    if j == 2:
                        gp.wait_ge(w_turned, 8)
                    gp.tensor_scalar(w_int_rows, w_stage[j - 1], 1.0, -ROUND_ANY, ALU.mult, ALU.add).then_inc(w_int, 1)

            batches(gp, phase_a)
            second_stats(NB - 1, XS - 1)

            def outputs(b, n):
                gp.wait_ge(bias_added, b + 1)
                for i in range(NI):
                    gp.wait_ge(acc_read, b * NI + i + 1)
                    gp.tensor_tensor(x2t[n][:, i, :], x2t[n][:, i, :], ot[:, i % OT, :], ALU.add).then_inc(out_ready, 1)

            def phase_c(b, n, g):
                gp.wait_ge(x2c_loaded[n], (g + 1) * 16)
                if is_first(b):
                    gp.wait_ge(out_scales, 1)
                for i in range(NI):
                    last = gp.tensor_tensor(x2t[n][:, i, :], x2t[n][:, i, :], bq2_bc[:, :], ALU.add)
                last.then_inc(bias_added, 1)
                if not is_first(b):
                    outputs(b - 1, 1 - n)

            pairs(gp, phase_c)
            outputs(NB - 1, 1)

        @block.scalar
        def _(act):
            def scale_scan(j, n):
                act.wait_ge(stats1_ready, j + 1)
                for i in range(NI):
                    act.wait_ge(scan_ready, j * NI + i + 1)
                    wait_count(act, x2_done, (j - 2) * NI + i + 1)
                    act.activation(rs[n % 2][:, i, :], ps[:, i, :], ACT.Copy, scale=rstd1[:, n, i:i + 1]).then_inc(scan_scaled, 1)

            def weights(w):
                act.wait_ge(w_scale, w + 1)
                if w == 0:
                    act.wait_ge(consts_ready, 1)
                rows = (NF, KD)[w]
                stage = w_stage[w].rearrange("p (c d) -> p c d", c=rows)
                for c in range(rows):
                    last = act.activation(stage[:, c, :], stage[:, c, :], ACT.Identity, bias=round_any[:, :], scale=isw[w][:, c:c + 1])
                last.then_inc(w_shifted, 1)
                if w == 0:
                    act.wait_ge(b_turned, 1)
                    act.activation(b1c[:, :], ps[:, 7, 0:NF], ACT.Copy)
                    act.activation(b2c[:, :], ps[:, 7, NF:NF + KD], ACT.Copy).then_inc(b_kept, 1)
                whole = (w1T, w2T)[w][:, :, :].rearrange("p a b -> p (a b)")
                for h in range(8):
                    act.wait_ge(w_turned, 8 * w + h + 1)
                    act.activation(whole[:, h * 1024:(h + 1) * 1024], ps[:, 4 + h % 4, :].bitcast(BF16), ACT.Copy).then_inc(w_kept, 1)

            def phase_a(j, n, g):
                act.wait_ge(ctx_loaded[n], (g + 1) * 16)
                act.activation(ct[n], ct[n], ACT.Square).then_inc(ctx_squared, 1)
                if not is_first(j):
                    scale_scan(j - 1, (n - 1) % XS)
                if isinstance(j, int) and j in (1, 2):
                    weights(j - 1)

            batches(act, phase_a)
            scale_scan(NB - 1, XS - 1)

            def phase_b(b, n, g):
                act.wait_ge(x2_loaded[n], (g + 1) * 16)
                if is_first(b):
                    act.wait_ge(q_scales, 1)
                for i in range(NI):
                    u = b * NI + i
                    last = act.activation(x2t[n][:, i, :], x2t[n][:, i, :], ACT.Relu, bias=qb[:, bass.ds(u, 1)], scale=qa[:, bass.ds(u, 1)])
                last.then_inc(x_scaled, 1)
                if is_first(b):
                    for m in range(XS):
                        act.wait_ge(x2_stored[m], 16 * NG)
                act.wait_ge(x_turned, b + 1)
                act.activation(xq[:, bass.ds(b * (KD * S), KD * S)], tp_banks(n), ACT.Copy).then_inc(xq_kept, 1)

            pairs(act, phase_b)
            act.wait_ge(h_scales, 1)

            def phase_c(b):
                for f in range(NF):
                    act.wait_ge(h_ready, b * NF + f + 1)
                    wait_count(act, h_int, b * NF + f - HV + 1)
                    act.activation(hv[:, f % HV, :], ps[:, f % HV, :], ACT.Relu, bias=hb[:, f:f + 1], scale=hs[:, f:f + 1]).then_inc(h_scaled, 1)

            singles(act, phase_c)

        @block.vector
        def _(dve):
            chained = [0]

            def link(ins):
                chained[0] += 1
                ins.then_inc(dve_step, 1)
                dve.wait_ge(dve_step, chained[0])

            dve.wait_ge(consts_ready, 1)
            link(dve.tensor_tensor_scan(decay_mat, decays, impulse, 0.0, ALU.mult, ALU.add))

            def weights(w):
                rows = (NF, KD)[w]
                dve.wait_ge(w_loaded[w], 16)
                link(dve.tensor_reduce(wmax[w][:, :], w_stage[w].rearrange("p (c d) -> p c d", c=rows), AX.X, ALU.max,
                                       apply_absolute_value=True))
                link(dve.tensor_scalar(sw[w][:, :], wmax[w][:, :], Q_EPS, 1.0 / 127.0, ALU.max, ALU.mult))
                dve.reciprocal(isw[w][:, :], sw[w][:, :]).then_inc(w_scale, 1)

            def make_x2(j, n):
                dve.wait_ge(stats1_ready, j + 1)

                def product(i):
                    dve.wait_ge(scan_scaled, j * NI + i + 1)
                    dve.scalar_tensor_tensor(rs[n % 2][:, i, :], xt[n][:, i, :], mean1[:, n, i:i + 1], rs[n % 2][:, i, :],
                                             ALU.subtract, ALU.mult).then_inc(prod_done, 1)

                def stats(i):
                    dve.wait_ge(x2_done, j * NI + i + 1)
                    return dve.bn_stats(st2[:, n, i, :], xt[n][:, i, :])

                def add(i):
                    dve.tensor_tensor_reduce(xt[n][:, i, :], rs[n % 2][:, i, :], xt[n][:, i, :], 1.0, -3.0e38, ALU.add, ALU.max,
                                             rowmax[:, n, i:i + 1]).then_inc(x2_done, 1)

                product(0)
                product(1)
                dve.wait_ge(prod_done, j * NI + 1)
                product(2)
                add(0)
                dve.wait_ge(prod_done, j * NI + 2)
                product(3)
                add(1)
                dve.wait_ge(prod_done, j * NI + 3)
                stats(0)
                add(2)
                dve.wait_ge(prod_done, j * NI + 4)
                stats(1)
                add(3)
                stats(2)
                stats(3).then_inc(stats2_in, 1)

            def phase_a(j, n, g):
                dve.wait_ge(x_loaded[n], (g + 1) * 16)
                for i in range(NI):
                    last = dve.bn_stats(st1[:, n, i, :], xt[n][:, i, :])
                last.then_inc(stats1_in, 1)
                if isinstance(j, int) and j in (1, 2):
                    weights(j - 1)
                if not is_first(j):
                    make_x2(j - 1, (n - 1) % XS)

            batches(dve, phase_a)
            make_x2(NB - 1, XS - 1)

            def over_partitions(col, spread):
                dve.tensor_scalar(diag[:, :], ident[:, :], col, None, ALU.mult).then_inc(diag_ready, 1)
                dve.wait_ge(spread_ready, spread)
                link(dve.tensor_reduce(cmax[:, 1:2], ps[:, 4, 0:P], AX.X, ALU.max))

            def round_bias(b, cs, bq):
                w = b.shape[1]
                t = [rb[:, k, 0:w] for k in range(10)]
                link(dve.reciprocal(t[0], cs))
                link(dve.tensor_tensor(t[1], b, t[0], ALU.mult))
                link(dve.tensor_scalar(t[2], t[1], -ROUND_POS, ROUND_POS, ALU.max, ALU.min))
                link(dve.tensor_scalar(t[3], t[2], 0.0, ROUND_POS, ALU.max, ALU.add))
                link(dve.tensor_scalar(t[4], t[3], ROUND_POS, None, ALU.subtract))
                link(dve.tensor_scalar(t[5], t[2], 0.0, ROUND_POS, ALU.min, ALU.subtract))
                link(dve.tensor_scalar(t[6], t[5], ROUND_POS, None, ALU.add))
                link(dve.tensor_tensor(t[7], t[1], t[2], ALU.subtract))
                link(dve.tensor_tensor(t[8], t[4], t[6], ALU.add))
                link(dve.tensor_tensor(t[9], t[8], t[7], ALU.add))
                link(dve.tensor_tensor(bq, t[9], cs, ALU.mult))

            dve.wait_ge(stats2_ready, NB)
            link(dve.tensor_tensor(zrow[:, :], zrow[:, :], rstd2[:, :], ALU.mult))
            link(dve.tensor_reduce(cmax[:, 0:1], zrow[:, :], AX.X, ALU.max))
            over_partitions(cmax[:, 0:1], 1)
            link(dve.tensor_scalar(s1[:, :], cmax[:, 1:2], Q_EPS, 1.0 / 255.0, ALU.max, ALU.mult))
            link(dve.reciprocal(is1[:, :], s1[:, :]))
            link(dve.tensor_scalar(qa[:, :], rstd2[:, :], is1[:, 0:1], None, ALU.mult))
            dve.scalar_tensor_tensor(qb[:, :], mean2[:, :], -1.0, qa[:, :], ALU.mult, ALU.mult).then_inc(q_scales, 1)
            link(dve.tensor_scalar(cs1[:, :], sw[0][:, :], s1[:, 0:1], None, ALU.mult))
            dve.wait_ge(b_kept, 1)
            round_bias(b1c[:, :], cs1[:, :], bq1[:, :])

            def hidden_max(b):
                for m in range(NF // 2):
                    dve.wait_ge(hid_ready, b * (NF // 2) + m + 1)
                    dve.tensor_reduce(hmax[:, bass.ds(b * NF + 2 * m, 2)], ps[:, 2 * (m % 2):2 * (m % 2) + 2, :],
                                      AX.X, ALU.max).then_inc(hid_maxed, 1)

            def phase_b(b, n, g):
                dve.wait_ge(x_scaled, b + 1)
                wait_count(dve, x_turned, b - 1)
                dve.tensor_scalar(qi[n], x2t[n], ROUND_POS, ROUND_POS, ALU.add, ALU.subtract).then_inc(x_int, 1)
                if not is_first(b):
                    hidden_max(b - 1)

            pairs(dve, phase_b)
            hidden_max(NB - 1)

            dve.wait_ge(hid_maxed, NB * NF // 2)
            link(dve.tensor_reduce(hm[:, 0, :], hmax.rearrange("p (b f) -> p f b", f=NF), AX.X, ALU.max))
            link(dve.tensor_tensor(hm[:, 1, :], hm[:, 0, :], cs1[:, :], ALU.mult))
            link(dve.tensor_tensor(hm[:, 2, :], hm[:, 1, :], bq1[:, :], ALU.add))
            link(dve.tensor_reduce(cmax[:, 2:3], hm[:, 2, :], AX.X, ALU.max))
            link(dve.tensor_scalar(cmax[:, 3:4], cmax[:, 2:3], 0.0, None, ALU.max))
            over_partitions(cmax[:, 3:4], 2)
            link(dve.tensor_scalar(s2[:, :], cmax[:, 1:2], Q_EPS, 1.0 / 255.0, ALU.max, ALU.mult))
            link(dve.reciprocal(is2[:, :], s2[:, :]))
            dve.tensor_scalar(hs[:, :], cs1[:, :], is2[:, 0:1], None, ALU.mult)
            dve.tensor_scalar(hb[:, :], bq1[:, :], is2[:, 0:1], None, ALU.mult).then_inc(h_scales, 1)
            link(dve.tensor_scalar(cs2[:, :], sw[1][:, :], s2[:, 0:1], None, ALU.mult))
            round_bias(b2c[:, :], cs2[:, :], bq2[:, :])
            for k in range(KD):
                dve.tensor_scalar(diag_cs[:, k * P:(k + 1) * P], ident[:, :], cs2[:, k:k + 1], None, ALU.mult)
                last = dve.tensor_scalar(diag_bq[:, k * P:(k + 1) * P], ident[:, :], bq2[:, k:k + 1], None, ALU.mult)
            last.then_inc(diag_ready, 1)
            dve.wait_ge(spread_ready, 3)
            dve.tensor_copy(cs2_bc[:, :], ps[:, 5, :])
            dve.tensor_copy(bq2_bc[:, :], ps[:, 6, :]).then_inc(out_scales, 1)
            dve.wait_ge(out_scales, 1)

            def scale_out(b):
                for i in range(NI):
                    dve.wait_ge(acc_ready, b * NI + i + 1)
                    wait_count(dve, out_ready, b * NI + i - OT + 1)
                    dve.tensor_tensor(ot[:, i % OT, :], ps[:, 4 + i, :], cs2_bc[:, :], ALU.mult).then_inc(acc_read, 1)

            def phase_c(b):
                for f in range(NF):
                    if f == 3 and not is_first(b):
                        scale_out(b - 1)
                    dve.wait_ge(h_scaled, b * NF + f + 1)
                    if f < HQ - 1:
                        wait_count(dve, hq_used, (b - 1) * (NF - 1) + f + HQ + 1)
                    elif f == HQ - 1:
                        wait_count(dve, acc_ready, b * NI)
                    else:
                        dve.wait_ge(hq_used, b * (NF - 1) + f - HQ + 1)
                    dve.tensor_scalar(hq[:, f % HQ, :], hv[:, f % HV, :], ROUND_POS, ROUND_POS, ALU.add, ALU.subtract).then_inc(h_int, 1)

            singles(dve, phase_c, straight=2)
            scale_out(NB - 1)

        @block.tensor
        def _(pe):
            def weights(w):
                pe.wait_ge(w_int, w + 1)
                if w == 0:
                    pe.wait_ge(b_loaded, 32)
                    pe.transpose(ps[:, 7, 0:NF], brow[:, :], ident[0:NF, 0:NF])
                    pe.transpose(ps[:, 7, NF:NF + KD], brow2[:, :], ident[0:KD, 0:KD]).then_inc(b_turned, 1)
                    pe.wait_ge(b_kept, 1)
                for h in range(8):
                    wait_count(pe, w_kept, 8 * w + h - 3)
                    bank = ps[:, 4 + h % 4, :].bitcast(BF16)
                    for n in range(8):
                        if w == 0:
                            at = (8 * (h % 2) + n) * D + (h // 2) * P
                        else:
                            at = (n % KD) * F + (2 * h + n // KD) * P
                        last = pe.transpose(bank[:, n * P:(n + 1) * P], w_int_rows[:, at:at + P], ident_b[:, :])
                    last.then_inc(w_turned, 1)

            def phase_a(j, n, g):
                pe.wait_ge(ctx_squared, j + 1)
                if is_first(j):
                    pe.wait_ge(dve_step, 1)
                for i in range(NI):
                    wait_count(pe, scan_scaled, (j - 1) * NI + i + 1)
                    for k in range(i + 1):
                        last = pe.matmul(ps[:, i, :], decay_mat[:, (i - k) * P:(i - k + 1) * P], ct[n][:, k, :],
                                         start=(k == 0), stop=(k == i))
                    last.then_inc(scan_ready, 1)
                if isinstance(j, int) and j in (1, 2):
                    weights(j - 1)

            batches(pe, phase_a)

            def spread(turn):
                pe.wait_ge(diag_ready, turn)
                pe.matmul(ps[:, 4, 0:P], ones[:, :], diag[:, :], start=True, stop=True).then_inc(spread_ready, 1)

            spread(1)

            def first_product(bank, b, f):
                for k in range(KD):
                    last = pe.matmul(ps[:, bank, :], w1T[:, k, f * P:(f + 1) * P], xq[:, bass.ds(b * (KD * S) + k * S, S)],
                                     start=(k == 0), stop=(k == KD - 1))
                return last

            def hidden(b, m):
                if m == 0:
                    pe.wait_ge(xq_kept, b + 1)
                wait_count(pe, hid_maxed, b * (NF // 2) + m - 1)
                first_product(2 * (m % 2), b, 2 * m)
                first_product(2 * (m % 2) + 1, b, 2 * m + 1).then_inc(hid_ready, 1)

            def turn_x(b, n):
                pe.wait_ge(x_int, b + 1)
                wait_count(pe, xq_kept, b - 1)
                for k in range(KD):
                    for i in range(NI):
                        last = pe.transpose(tp_banks(n)[:, k * S + i * P:k * S + (i + 1) * P], qi[n][:, i, k * P:(k + 1) * P], ident_b[:, :])
                last.then_inc(x_turned, 1)

            def phase_b(b, n, g):
                if not is_first(b):
                    for m in range(NF // 4):
                        hidden(b - 1, m)
                turn_x(b, n)
                if not is_first(b):
                    for m in range(NF // 4, NF // 2):
                        hidden(b - 1, m)

            pairs(pe, phase_b)
            for m in range(NF // 2):
                hidden(NB - 1, m)
            spread(2)

            def hidden_chunk(b, f):
                wait_count(pe, h_scaled, b * NF + f - HV + 1)
                first_product(f % HV, b, f).then_inc(h_ready, 1)

            def second_product(b, f):
                pe.wait_ge(h_int, b * NF + f + 1)
                for i in range(NI):
                    if f == 0:
                        wait_count(pe, acc_read, (b - 1) * NI + i + 1)
                    last = pe.matmul(ps[:, 4 + i, :], hq[:, f % HQ, i * P:(i + 1) * P], w2T[:, f, :],
                                     start=(f == 0), stop=(f == NF - 1))
                    if f == NF - 1:
                        last.then_inc(acc_ready, 1)
                if f < NF - 1:
                    last.then_inc(hq_used, 1)

            LAG = 4

            def phase_c(b):
                for f in range(NF):
                    hidden_chunk(b, f)
                    if f < LAG - 1:
                        if not is_first(b):
                            second_product(b - 1, NF - LAG + 1 + f)
                    elif f >= LAG:
                        second_product(b, f - LAG)
                    if is_first(b) and f == LAG - 1:
                        pe.wait_ge(diag_ready, 3)
                        pe.matmul(ps[:, 5, :], ones[:, :], diag_cs, start=True, stop=True)
                        pe.matmul(ps[:, 6, :], ones[:, :], diag_bq, start=True, stop=True).then_inc(spread_ready, 1)
                        pe.wait_ge(out_scales, 1)
                second_product(b, NF - LAG)

            pe.wait_ge(hid_maxed, NB * NF // 2)
            singles(pe, phase_c)
            for f in range(NF - LAG + 1, NF):
                second_product(NB - 1, f)


_INS = ["x", "ctx_1024", "L0_ffn_w1", "L0_ffn_b1", "L0_ffn_w2", "L0_ffn_b2"]


def kernel(**inputs):
    import numpy as _np
    import concourse.bacc as _bacc
    from concourse import mybir as _mybir
    from concourse.bass_utils import run_bass_kernel_spmd as _run

    nc = _bacc.Bacc("TRN2", target_bir_lowering=False, num_devices=1)
    arrays, args = {}, []
    for name in _INS:
        a = _np.ascontiguousarray(inputs[name])
        arrays[f"in_{name}_dram"] = a
        args.append(nc.dram_tensor(f"in_{name}_dram", a.shape, _mybir.dt.from_np(a.dtype), kind="ExternalInput").ap())
    shape = arrays["in_x_dram"].shape
    args.append(nc.dram_tensor("out_0_dram", shape, _mybir.dt.float32, kind="ExternalOutput").ap())
    build(nc, *args)
    r = _run(nc, [arrays], core_ids=[0])
    return r.results[0]["out_0_dram"]
```

```python
from contextlib import ExitStack

import concourse.bass as bass
from concourse import mybir

ALU = mybir.AluOpType
ACT = mybir.ActivationFunctionType
AX = mybir.AxisListType
F32 = mybir.dt.float32
BF16 = mybir.dt.bfloat16

P = 128
BANK = 512
DECAY = 0.9
LN_EPS = 1e-5
Q_EPS = 1e-8
ROUND_POS = 2.0 ** 23
ROUND_ANY = 1.5 * 2.0 ** 23
XS = 4
HQ = 8
HV = 2
HB = 4
KEPT = 4
ACT_TILES = 2
BEFORE = 4
AHEAD = 2


def wait_count(eng, sem, count):
    if isinstance(count, int) and count <= 0:
        return
    eng.wait_ge(sem, count)


def build(nc, x, ctx_in, w1, b1, w2, b2, out):
    NB, S, D = x.shape
    F = w1.shape[0]
    NI = S // P
    KD = D // P
    NF = F // P
    NU = NB * NI
    ROW = NI * D
    NP2 = NF // 2
    NC = NF - 2 * KEPT

    def spread_over(n, k):
        return [(q + 1) * k // n > q * k // n for q in range(n)]

    kept_b = spread_over(NP2, KEPT)
    order_b = [(NC // 2 + sum(kept_b[:q])) if kept_b[q] else q - sum(kept_b[:q]) for q in range(NP2)]
    kept_c = spread_over(NF, 2 * KEPT)
    order_c = [(NC + sum(kept_c[:q])) if kept_c[q] else q - sum(kept_c[:q]) for q in range(NF)]
    place_c = {f: q for q, f in enumerate(order_c)}
    assert D == BANK and S == BANK and NI == KD == 4 and NF % HQ == 0 and NB % XS == 0

    x_rows = x.rearrange("b (i p) d -> b p i d", p=P)
    ctx_rows = ctx_in.rearrange("b (i p) d -> b p i d", p=P)
    out_rows = out.rearrange("b (i p) d -> b p i d", p=P)
    w1_rows = w1.rearrange("(c p) d -> p c d", p=P)
    w2_rows = w2.rearrange("(k p) f -> p k f", p=P)
    b1_rows = b1.rearrange("(c p) -> c p", p=P)
    b2_rows = b2.rearrange("(k p) -> k p", p=P)
    h_dram = nc.dram_tensor("hidden_scratch", [NB, KEPT, P, 2 * S], F32, kind="Internal").ap()
    x2_dram = nc.dram_tensor("x2_scratch", [NB, P, ROW], F32, kind="Internal").ap()

    with ExitStack() as es:
        def sb(name, shape, dt=F32):
            return es.enter_context(nc.sbuf_tensor(name, shape, dt))

        def sem(name):
            return es.enter_context(nc.semaphore(name))

        xq = sb("xq", [P, NB * KD * S], BF16)
        arena = xq[:, :].bitcast(F32)
        o = NF * D + NF * D // 2
        rs = [arena[:, o + n * ROW:o + (n + 1) * ROW].rearrange("p (i d) -> p i d", i=NI) for n in range(2)]
        o += 2 * ROW
        ct = [arena[:, o + n * ROW:o + (n + 1) * ROW].rearrange("p (i d) -> p i d", i=NI) for n in range(XS)]
        o += XS * ROW
        xt = [arena[:, o + n * ROW:o + (n + 1) * ROW].rearrange("p (i d) -> p i d", i=NI) for n in range(XS)]
        assert o + XS * ROW == NB * KD * S // 2

        w1T = sb("w1T", [P, KD, F], BF16)
        w2T = sb("w2T", [P, NF, D], BF16)
        ident = sb("ident", [P, P])
        ident_b = sb("ident_b", [P, P], BF16)
        ones = sb("ones", [P, P])
        diag = sb("diag", [P, P])
        st1 = sb("st1", [P, XS, NI, 6])
        st2 = sb("st2", [P, XS, NI, 6])
        rowmax = sb("rowmax", [P, XS, NI])
        pw1 = sb("pw1", [P, 8, NI])
        pw2 = sb("pw2", [P, 10, XS * NI])
        half = sb("half", [P, XS * NI])
        neg_half = sb("neg_half", [P, XS * NI])
        per_row = sb("per_row", [P, XS * NI])
        eps = sb("eps", [P, XS * NI])
        mean1 = sb("mean1", [P, XS, NI])
        rstd1 = sb("rstd1", [P, XS, NI])
        mean2 = sb("mean2", [P, NU])
        rstd2 = sb("rstd2", [P, NU])
        zrow = sb("zrow", [P, NU])
        qa = zrow
        qb = sb("qb", [P, NU])
        minus_round = sb("minus_round", [P, 1])
        wmax = [sb("wmax1", [P, NF]), sb("wmax2", [P, KD])]
        sw = [sb("sw1", [P, NF]), sb("sw2", [P, KD])]
        isw = [sb("isw1", [P, NF]), sb("isw2", [P, KD])]
        brow = sb("brow", [NF, P])
        brow2 = sb("brow2", [KD, P])
        b1c = sb("b1c", [P, NF])
        b2c = sb("b2c", [P, KD])
        rb = pw2
        s1 = sb("s1", [P, 1])
        is1 = sb("is1", [P, 1])
        s2 = sb("s2", [P, 1])
        is2 = sb("is2", [P, 1])
        cmax = sb("cmax", [P, 6])
        cs1 = sb("cs1", [P, NF])
        bq1 = sb("bq1", [P, NF])
        hm = sb("hm", [P, 3, NF])
        hs = sb("hs", [P, NF])
        hb = sb("hb", [P, NF])
        cs2 = sb("cs2", [P, KD])
        bq2 = sb("bq2", [P, KD])
        cs2_bc = sb("cs2_bc", [P, D])
        bq2_bc = sb("bq2_bc", [P, D])
        work = sb("work", [P, 4 * ROW + 2 * D])
        x2t = [work[:, n * ROW:(n + 1) * ROW].rearrange("p (i d) -> p i d", i=NI) for n in range(2)]
        qi = [work[:, (4 + n) * ROW // 2:(5 + n) * ROW // 2].bitcast(BF16).rearrange("p (i d) -> p i d", i=NI) for n in range(2)]
        hkeep = [work[:, 3 * ROW + n * 2 * S:3 * ROW + (n + 1) * 2 * S].rearrange("p (n t) -> p n t", n=2) for n in range(2)]
        hmax = work[:, 4 * ROW:4 * ROW + NB * NF]
        x2c = work[:, 0:ROW].rearrange("p (i d) -> p i d", i=NI)
        hload = [work[:, ROW + n * 2 * S:ROW + (n + 1) * 2 * S].rearrange("p (n t) -> p n t", n=2) for n in range(2)]
        ot = work[:, 2 * ROW:3 * ROW].rearrange("p (i d) -> p i d", i=NI)
        hq = work[:, 3 * ROW:3 * ROW + HQ * S // 2].bitcast(BF16).rearrange("p (n t) -> p n t", n=HQ)
        hv = work[:, 4 * ROW:4 * ROW + HV * S].rearrange("p (n t) -> p n t", n=HV)
        decay_mat = work[:, 4 * ROW:4 * ROW + S]
        diag_cs, diag_bq = ot[:, 0, :], ot[:, 1, :]
        unused = work[:, 4 * ROW + S:4 * ROW + S + D]
        w_stage = [arena[:, 0:NF * D], work[:, 0:4 * ROW]]
        w_int_rows = arena[:, NF * D:NF * D + NF * D // 2].bitcast(BF16)
        decays, impulse = xt[XS - 1][:, 0, :], xt[XS - 1][:, 1, :]

        ps = es.enter_context(nc.psum_tensor("ps", [P, 8, BANK], F32))

        consts_ready = sem("consts_ready")
        gp_step = sem("gp_step")
        ln1_step = sem("ln1_step")
        ln2_step = sem("ln2_step")
        dve_step = sem("dve_step")
        act_step = sem("act_step")
        x_loaded = [sem(f"x_loaded{n}") for n in range(XS)]
        ctx_loaded = [sem(f"ctx_loaded{n}") for n in range(XS)]
        ctx_squared = sem("ctx_squared")
        scan_ready = sem("scan_ready")
        scan_scaled = sem("scan_scaled")
        stats1_in = sem("stats1_in")
        stats1_ready = sem("stats1_ready")
        prod_done = sem("prod_done")
        x2_done = sem("x2_done")
        stats2_in = sem("stats2_in")
        stats2_used = sem("stats2_used")
        stats2_ready = sem("stats2_ready")
        x2_stored = [sem(f"x2_stored{n}") for n in range(XS)]
        w_loaded = [[sem(f"w_loaded{w}{h}") for h in range(2)] for w in range(2)]
        b_loaded = sem("b_loaded")
        w_scale = sem("w_scale")
        w_rounded = sem("w_rounded")
        w_int = sem("w_int")
        w_turned = sem("w_turned")
        w_kept = sem("w_kept")
        b_turned = sem("b_turned")
        b_kept = sem("b_kept")
        diag_ready = sem("diag_ready")
        spread_ready = sem("spread_ready")
        q_scales = sem("q_scales")
        x2_loaded = [sem(f"x2_loaded{n}") for n in range(2)]
        x_scaled = sem("x_scaled")
        x_int = sem("x_int")
        x_turned = sem("x_turned")
        xq_kept = sem("xq_kept")
        hid_ready = sem("hid_ready")
        hid_maxed = sem("hid_maxed")
        h_scales = sem("h_scales")
        h_ready = sem("h_ready")
        h_scaled = sem("h_scaled")
        h_int = sem("h_int")
        acc_ready = sem("acc_ready")
        acc_read = sem("acc_read")
        out_scales = sem("out_scales")
        hq_used = sem("hq_used")
        h_copied = sem("h_copied")
        h_stored = [sem(f"h_stored{n}") for n in range(2)]
        h_loaded = [sem(f"h_loaded{n}") for n in range(2)]
        x2c_loaded = sem("x2c_loaded")
        bias_added = sem("bias_added")
        out_ready = sem("out_ready")
        out_stored = sem("out_stored")

        NG = NB // XS
        STRAIGHT = AHEAD * XS
        block = es.enter_context(nc.Block())

        def batches(eng, step, peeled=0):
            for j in range(STRAIGHT):
                step(j, j % XS, j // XS)
            with eng.Fori(AHEAD, NG - peeled) as g:
                for n in range(XS):
                    step(g * XS + n, n, g)
            for j in range(NB - peeled * XS, NB):
                step(j, j % XS, j // XS)

        def pairs(eng, step, straight=1):
            for t in range(2 * straight):
                step(t, t % 2, t // 2)
            with eng.Fori(straight, NB // 2) as g:
                for n in range(2):
                    step(g * 2 + n, n, g)

        def singles(eng, step, straight=1):
            for b in range(straight):
                step(b)
            with eng.Fori(straight, NB) as b:
                step(b)

        def is_first(j, n=1):
            return isinstance(j, int) and j < n

        def weight_halves(j):
            at = {1: (0, 0), 2: (0, 1), 4: (1, 0), 5: (1, 1)}.get(j) if isinstance(j, int) else None
            return [at] if at else []

        def weight_quarters(j):
            return [(w, 2 * h + n) for w, h in weight_halves(j - 1) for n in range(2)] if isinstance(j, int) else []

        def tp_banks(n):
            return ps[:, 4 + 2 * n:6 + 2 * n, :].rearrange("p n e -> p (n e)").bitcast(BF16)

        @block.sync
        def _(sp):
            def store_x2(j, n):
                sp.wait_ge(x2_done, (j + 1) * NI)
                sp.dma_start(x2_dram[bass.ds(j, 1)].rearrange("b p m -> (b p) m"),
                             xt[n].rearrange("p i d -> p (i d)")).then_inc(x2_stored[n], 16)

            def load_x2(t, n):
                sp.dma_start(x2t[n].rearrange("p i d -> p (i d)"),
                             x2_dram[bass.ds(t, 1)].rearrange("b p m -> (b p) m")).then_inc(x2_loaded[n], 16)

            def phase_a(j, n, g):
                if isinstance(j, int) and j == XS - 1:
                    sp.wait_ge(dve_step, 1)
                if not is_first(j, XS):
                    sp.wait_ge(x2_stored[n], g * 16)
                sp.dma_start(xt[n], x_rows[bass.ds(j, 1)].rearrange("b p i d -> (b p) i d")).then_inc(x_loaded[n], 16)
                for w, h in weight_halves(j):
                    rows = (NF, KD)[w]
                    part = slice(h * rows // 2, (h + 1) * rows // 2)
                    sp.dma_start(w_stage[w].rearrange("p (c d) -> p c d", c=rows)[:, part, :],
                                 (w1_rows, w2_rows)[w][:, part, :]).then_inc(w_loaded[w][h], 16)
                if isinstance(j, int) and j == 2:
                    sp.dma_start(brow[:, :], b1_rows).then_inc(b_loaded, 16)
                    sp.dma_start(brow2[:, :], b2_rows).then_inc(b_loaded, 16)
                if not is_first(j, 2):
                    store_x2(j - 2, (n - 2) % XS)

            batches(sp, phase_a)
            sp.wait_ge(w_int, 8)
            for t in range(2):
                load_x2(t, t)
            store_x2(NB - 2, XS - 2)
            store_x2(NB - 1, XS - 1)
            for n in range(XS):
                sp.wait_ge(x2_stored[n], 16 * NG)

            def store_kept(b, k):
                sp.wait_ge(h_copied, b * KEPT + k + 1)
                sp.dma_start(h_dram[bass.ds(b, 1), k].rearrange("b p m -> (b p) m"),
                             hkeep[k % 2].rearrange("p n t -> p (n t)")).then_inc(h_stored[k % 2], 16)

            def phase_b(t, n, g):
                if not is_first(t, 2):
                    sp.wait_ge(x_int, t - 1)
                    load_x2(t, n)
                if not is_first(t, 3):
                    for k in range(KEPT):
                        store_kept(t - 3, k)

            pairs(sp, phase_b, straight=2)
            for b in range(NB - 3, NB):
                for k in range(KEPT):
                    store_kept(b, k)
            for n in range(2):
                sp.wait_ge(h_stored[n], 16 * NB * KEPT // 2)

            def load_kept(b, k):
                if k >= 2:
                    sp.wait_ge(h_scaled, b * NF + place_c[NC + 2 * (k - 2) + 1] + 1)
                else:
                    wait_count(sp, h_scaled, (b - 1) * NF + place_c[NC + 2 * (k - 2 + KEPT) + 1] + 1)
                sp.dma_start(hload[k % 2].rearrange("p n t -> p (n t)"),
                             h_dram[bass.ds(b, 1), k].rearrange("b p m -> (b p) m")).then_inc(h_loaded[k % 2], 16)

            def store_out(b):
                sp.wait_ge(out_ready, (b + 1) * NI)
                sp.dma_start(out_rows[bass.ds(b, 1)].rearrange("b p i d -> (b p) i d"), x2c).then_inc(out_stored, 16)

            def phase_c(b):
                for k in range(KEPT - 1):
                    load_kept(b, k)
                if not is_first(b):
                    store_out(b - 1)
                load_kept(b, KEPT - 1)
                wait_count(sp, out_stored, b * 16)
                sp.dma_start(x2c.rearrange("p i d -> p (i d)"),
                             x2_dram[bass.ds(b, 1)].rearrange("b p m -> (b p) m")).then_inc(x2c_loaded, 16)

            singles(sp, phase_c)
            store_out(NB - 1)
            sp.wait_ge(out_stored, 16 * NB)

        @block.gpsimd
        def _(gp):
            gp.memset(minus_round[:, :], -ROUND_ANY)
            gp.memset(half[:, :], 0.5)
            gp.memset(per_row[:, :], 1.0 / D)
            gp.memset(eps[:, :], LN_EPS)
            gp.memset(ones[:, :], 1.0)
            gp.memset(decays, DECAY)
            gp.memset(neg_half[:, :], -0.5)
            gp.memset(impulse, 0.0)
            for n in range(XS):
                gp.memset(st1[:, n, NI - ACT_TILES:NI, 5:6], 0.0)
            gp.memset(ident[:, :], 0.0)
            gp.memset(ident_b[:, :], 0.0).then_inc(gp_step, 1)
            gp.wait_ge(gp_step, 1)
            for m, w in ((impulse, S), (ident[:, :], P), (ident_b[:, :], P)):
                last = gp.affine_select(out=m, in_=m, compare_op=ALU.not_equal, fill=1.0, base=0,
                                        pattern=[[-1, w]], channel_multiplier=1)
            last.then_inc(consts_ready, 1)

            def row_stats(pw, st, mean, done, base):
                n = st.shape[1]
                me, mo, ve, vo = (st[:, :, k] for k in (1, 4, 2, 5))
                t = [pw[:, k, :] for k in range(8)]
                gp.tensor_tensor(t[0], me, mo, ALU.add)
                gp.tensor_tensor(t[1], ve, vo, ALU.add)
                gp.tensor_tensor(t[2], me, mo, ALU.subtract).then_inc(done, 1)
                gp.wait_ge(done, base + 1)
                gp.tensor_tensor(mean, t[0], half[:, 0:n], ALU.mult)
                gp.tensor_tensor(t[3], t[1], per_row[:, 0:n], ALU.mult)
                gp.tensor_tensor(t[4], t[2], half[:, 0:n], ALU.mult).then_inc(done, 1)
                gp.wait_ge(done, base + 2)
                gp.tensor_tensor(t[5], t[3], eps[:, 0:n], ALU.add)
                gp.tensor_tensor(t[6], t[4], t[4], ALU.mult).then_inc(done, 1)
                gp.wait_ge(done, base + 3)
                gp.tensor_tensor(t[7], t[5], t[6], ALU.add).then_inc(done, 1)
                return t[7]

            def second_stats(g):
                cols = bass.ds(g * (XS * NI), XS * NI)
                wait_count(gp, stats2_ready, g)
                gp.wait_ge(stats2_in, (g + 1) * XS)
                mean = pw2[:, 8, :]
                var = row_stats(pw2, st2[:, :, :, :].rearrange("p n i k -> p (n i) k"), mean, ln2_step, g * 4)
                gp.wait_ge(ln2_step, g * 4 + 4)
                gp.tensor_tensor(pw2[:, 9, :], var, var, ALU.add)
                gp.tensor_tensor(zrow[:, cols], rowmax[:, :, :].rearrange("p n i -> p (n i)"), mean, ALU.subtract).then_inc(stats2_used, 1)
                gp.tensor_tensor(mean2[:, cols], pw2[:, 0, :], half[:, :], ALU.mult)
                gp.tensor_tensor(rstd2[:, cols], var, neg_half[:, :], ALU.pow).then_inc(stats2_ready, 1)

            def round_weights(w, k):
                gp.wait_ge(w_scale, 2 * w + k // 2 + 1)
                rows = (NF, KD)[w] // 4
                quarter = w_stage[w][:, k * 4 * D:(k + 1) * 4 * D]
                for c in range(rows):
                    row = quarter.rearrange("p (c d) -> p c d", c=rows)[:, c, :]
                    last = gp.tensor_scalar(row, row, isw[w][:, k * rows + c:k * rows + c + 1], ROUND_ANY, ALU.mult, ALU.add)
                last.then_inc(w_rounded, 1)

            def phase_a(j, n, g):
                wait_count(gp, stats1_ready, j)
                gp.wait_ge(stats1_in, j + 1)
                gp.wait_ge(act_step, (j + 1) * (2 * ACT_TILES))
                var = row_stats(pw1, st1[:, n], mean1[:, n, :], ln1_step, j * 4)
                gp.wait_ge(ln1_step, j * 4 + 4)
                gp.tensor_tensor(rstd1[:, n, :], var, neg_half[:, 0:NI], ALU.pow).then_inc(stats1_ready, 1)
                if n == 0 and not is_first(j, XS):
                    second_stats(g - 1)
                for w, k in weight_quarters(j):
                    round_weights(w, k)

            batches(gp, phase_a)
            second_stats(NG - 1)

        @block.scalar
        def _(act):
            def tile_stats(j, n, g):
                for m, i in enumerate(range(NI - ACT_TILES, NI)):
                    at = j * (2 * ACT_TILES) + 2 * m
                    if m == 0:
                        act.wait_ge(x_loaded[n], (g + 1) * 16)
                    wait_count(act, act_step, at)
                    mean = st1[:, n, i, 1:2]
                    act.activation(unused, xt[n][:, i, :], ACT.Copy, scale=1.0 / D, accum_out=mean).then_inc(act_step, 1)
                    act.wait_ge(act_step, at + 1)
                    act.activation(st1[:, n, i, 4:5], mean, ACT.Copy)
                    last = act.activation(unused, xt[n][:, i, :], ACT.Square, bias=mean, scale=-1.0, accum_out=st1[:, n, i, 2:3])
                    last.then_inc(act_step, 1)

            def scale_scan(j, n, tiles):
                if 0 in tiles:
                    act.wait_ge(stats1_ready, j + 1)
                for i in tiles:
                    act.wait_ge(scan_ready, j * NI + i + 1)
                    wait_count(act, x2_done, (j - 2) * NI + i + 1)
                    act.activation(rs[n % 2][:, i, :], ps[:, i, :], ACT.Copy, scale=rstd1[:, n, i:i + 1]).then_inc(scan_scaled, 1)

            def int_weights(w, k):
                act.wait_ge(w_rounded, 4 * w + k + 1)
                if w == 1:
                    act.wait_ge(w_turned, 2 * k + 2)
                span = slice(k * 4 * D, (k + 1) * 4 * D)
                act.activation(w_int_rows[:, span], w_stage[w][:, span], ACT.Identity, bias=minus_round[:, 0:1]).then_inc(w_int, 1)

            def keep_weights(w, k):
                if (w, k) == (0, 0):
                    act.wait_ge(b_turned, 1)
                    act.activation(b1c[:, :], ps[:, 7, 0:NF], ACT.Copy)
                    act.activation(b2c[:, :], ps[:, 7, NF:NF + KD], ACT.Copy).then_inc(b_kept, 1)
                for h in range(2):
                    act.wait_ge(w_turned, 8 * w + 2 * k + h + 1)
                    bank = ps[:, 4 + (2 * k + h) % 4, :].bitcast(BF16)
                    if w == 0:
                        act.activation(w1T[:, 2 * h:2 * h + 2, k * 4 * P:(k + 1) * 4 * P], bank.rearrange("p (a f) -> p a f", a=2),
                                       ACT.Copy).then_inc(w_kept, 1)
                    else:
                        act.activation(w2T[:, 8 * h:8 * h + 8, k * P:(k + 1) * P], bank.rearrange("p (a f) -> p a f", a=8),
                                       ACT.Copy).then_inc(w_kept, 1)

            def load_ctx(j, n):
                act.dma_start(ct[n], ctx_rows[bass.ds(j, 1)].rearrange("b p i d -> (b p) i d")).then_inc(ctx_loaded[n], 16)

            def phase_a(j, n, g):
                if is_first(j):
                    for m in range(XS):
                        load_ctx(m, m)
                act.wait_ge(ctx_loaded[n], (g + 1) * 16)
                act.activation(ct[n], ct[n], ACT.Square).then_inc(ctx_squared, 1)
                if not is_first(j):
                    scale_scan(j - 1, (n - 1) % XS, range(BEFORE))
                tile_stats(j, n, g)
                if not is_first(j):
                    scale_scan(j - 1, (n - 1) % XS, range(BEFORE, NI))
                    if not (isinstance(j, int) and j - 1 + XS >= NB):
                        load_ctx(j - 1 + XS, (n - 1) % XS)
                if isinstance(j, int):
                    for w, k in weight_quarters(j - 1):
                        int_weights(w, k)
                    for w, k in weight_quarters(j - 3):
                        if w == 0:
                            keep_weights(w, k)

            batches(act, phase_a, peeled=1)
            scale_scan(NB - 1, XS - 1, range(NI))
            for k in range(4):
                keep_weights(1, k)

            def keep_sums(b, places):
                for q in places:
                    if kept_b[q]:
                        k = order_b[q] - NC // 2
                        act.wait_ge(hid_ready, b * NP2 + q + 1)
                        if k >= 2:
                            qf = order_b.index(NC // 2 + k - 2)
                            act.wait_ge(hid_maxed, b * NP2 + qf + 1)
                            act.wait_ge(h_stored[k % 2], b * (8 * KEPT) + 16 * (k // 2))
                        elif not is_first(b):
                            qf = order_b.index(NC // 2 + k - 2 + KEPT)
                            act.wait_ge(hid_maxed, (b - 1) * NP2 + qf + 1)
                            act.wait_ge(h_stored[k % 2], b * (8 * KEPT))
                        act.activation(hkeep[k % 2], ps[:, 2 * (q % 2):2 * (q % 2) + 2, :], ACT.Copy).then_inc(h_copied, 1)

            def phase_b(t, n, g):
                for i in range(NI):
                    if not is_first(t, 2):
                        keep_sums(t - 2, range(i * NP2 // NI, (i + 1) * NP2 // NI))
                    if i == 0:
                        act.wait_ge(x2_loaded[n], (g + 1) * 16)
                    if i == 0 and is_first(t):
                        act.wait_ge(q_scales, 1)
                    u = t * NI + i
                    last = act.activation(x2t[n][:, i, :], x2t[n][:, i, :], ACT.Relu, bias=qb[:, bass.ds(u, 1)], scale=qa[:, bass.ds(u, 1)])
                last.then_inc(x_scaled, 1)

            pairs(act, phase_b, straight=2)
            keep_sums(NB - 2, range(NP2))
            keep_sums(NB - 1, range(NP2))
            act.wait_ge(h_scales, 1)

            def phase_c(b):
                for q, f in enumerate(order_c):
                    wait_count(act, h_int, b * NF + q - HV + 1)
                    if kept_c[q]:
                        k, half_of = divmod(f - NC, 2)
                        act.wait_ge(h_loaded[k % 2], b * (8 * KEPT) + 16 * (k // 2 + 1))
                        src = hload[k % 2][:, half_of, :]
                    else:
                        act.wait_ge(h_ready, b * NC + f + 1)
                        src = ps[:, f % HB, :]
                    act.activation(hv[:, q % HV, :], src, ACT.Relu, bias=hb[:, f:f + 1], scale=hs[:, f:f + 1]).then_inc(h_scaled, 1)

            singles(act, phase_c)

        @block.vector
        def _(dve):
            chained = [0]

            def link(ins):
                chained[0] += 1
                ins.then_inc(dve_step, 1)
                dve.wait_ge(dve_step, chained[0])

            dve.wait_ge(consts_ready, 1)
            link(dve.tensor_tensor_scan(decay_mat, decays, impulse, 0.0, ALU.mult, ALU.add))

            def weight_scales(w, h):
                rows = (NF, KD)[w]
                part = slice(h * rows // 2, (h + 1) * rows // 2)
                dve.wait_ge(w_loaded[w][h], 16)
                link(dve.tensor_reduce(wmax[w][:, part], w_stage[w].rearrange("p (c d) -> p c d", c=rows)[:, part, :], AX.X,
                                       ALU.max, apply_absolute_value=True))
                link(dve.tensor_scalar(sw[w][:, part], wmax[w][:, part], Q_EPS, 1.0 / 127.0, ALU.max, ALU.mult))
                dve.reciprocal(isw[w][:, part], sw[w][:, part]).then_inc(w_scale, 1)

            def make_x2(j, n, g):
                dve.wait_ge(stats1_ready, j + 1)

                def product(i):
                    dve.wait_ge(scan_scaled, j * NI + i + 1)
                    dve.scalar_tensor_tensor(rs[n % 2][:, i, :], xt[n][:, i, :], mean1[:, n, i:i + 1], rs[n % 2][:, i, :],
                                             ALU.subtract, ALU.mult).then_inc(prod_done, 1)

                def stats(i):
                    dve.wait_ge(x2_done, j * NI + i + 1)
                    return dve.bn_stats(st2[:, n, i, :], xt[n][:, i, :])

                def add(i):
                    dve.tensor_tensor_reduce(xt[n][:, i, :], rs[n % 2][:, i, :], xt[n][:, i, :], 1.0, -3.0e38, ALU.add, ALU.max,
                                             rowmax[:, n, i:i + 1]).then_inc(x2_done, 1)

                product(0)
                product(1)
                if n == 0:
                    wait_count(dve, stats2_used, g)
                dve.wait_ge(prod_done, j * NI + 1)
                product(2)
                add(0)
                dve.wait_ge(prod_done, j * NI + 2)
                product(3)
                add(1)
                dve.wait_ge(prod_done, j * NI + 3)
                stats(0)
                add(2)
                dve.wait_ge(prod_done, j * NI + 4)
                stats(1)
                add(3)
                stats(2)
                stats(3).then_inc(stats2_in, 1)

            def phase_a(j, n, g):
                dve.wait_ge(x_loaded[n], (g + 1) * 16)
                for i in range(NI - ACT_TILES):
                    last = dve.bn_stats(st1[:, n, i, :], xt[n][:, i, :])
                last.then_inc(stats1_in, 1)
                if not is_first(j):
                    make_x2(j - 1, (n - 1) % XS, g - 1 if n == 0 else g)
                for w, h in weight_halves(j):
                    weight_scales(w, h)

            batches(dve, phase_a)
            make_x2(NB - 1, XS - 1, NG - 1)

            def over_partitions(col, spread):
                dve.tensor_scalar(diag[:, :], ident[:, :], col, None, ALU.mult).then_inc(diag_ready, 1)
                dve.wait_ge(spread_ready, spread)
                link(dve.tensor_reduce(cmax[:, 1:2], ps[:, 4, 0:P], AX.X, ALU.max))

            def round_bias(b, cs, bq):
                w = b.shape[1]
                t = [rb[:, k, 0:w] for k in range(10)]
                link(dve.reciprocal(t[0], cs))
                link(dve.tensor_tensor(t[1], b, t[0], ALU.mult))
                link(dve.tensor_scalar(t[2], t[1], -ROUND_POS, ROUND_POS, ALU.max, ALU.min))
                link(dve.tensor_scalar(t[3], t[2], 0.0, ROUND_POS, ALU.max, ALU.add))
                link(dve.tensor_scalar(t[4], t[3], ROUND_POS, None, ALU.subtract))
                link(dve.tensor_scalar(t[5], t[2], 0.0, ROUND_POS, ALU.min, ALU.subtract))
                link(dve.tensor_scalar(t[6], t[5], ROUND_POS, None, ALU.add))
                link(dve.tensor_tensor(t[7], t[1], t[2], ALU.subtract))
                link(dve.tensor_tensor(t[8], t[4], t[6], ALU.add))
                link(dve.tensor_tensor(t[9], t[8], t[7], ALU.add))
                link(dve.tensor_tensor(bq, t[9], cs, ALU.mult))

            dve.wait_ge(stats2_ready, NG)
            link(dve.tensor_tensor(zrow[:, :], zrow[:, :], rstd2[:, :], ALU.mult))
            link(dve.tensor_reduce(cmax[:, 0:1], zrow[:, :], AX.X, ALU.max))
            over_partitions(cmax[:, 0:1], 1)
            link(dve.tensor_scalar(s1[:, :], cmax[:, 1:2], Q_EPS, 1.0 / 255.0, ALU.max, ALU.mult))
            link(dve.reciprocal(is1[:, :], s1[:, :]))
            link(dve.tensor_scalar(qa[:, :], rstd2[:, :], is1[:, 0:1], None, ALU.mult))
            dve.scalar_tensor_tensor(qb[:, :], mean2[:, :], -1.0, qa[:, :], ALU.mult, ALU.mult).then_inc(q_scales, 1)
            link(dve.tensor_scalar(cs1[:, :], sw[0][:, :], s1[:, 0:1], None, ALU.mult))
            dve.wait_ge(b_kept, 1)
            round_bias(b1c[:, :], cs1[:, :], bq1[:, :])

            def hidden_max(b, places):
                for q in places:
                    if kept_b[q]:
                        k = order_b[q] - NC // 2
                        dve.wait_ge(h_copied, b * KEPT + k + 1)
                        sums = hkeep[k % 2]
                    else:
                        dve.wait_ge(hid_ready, b * NP2 + q + 1)
                        sums = ps[:, 2 * (q % 2):2 * (q % 2) + 2, :]
                    dve.tensor_reduce(hmax[:, bass.ds(b * NF + 2 * order_b[q], 2)], sums, AX.X, ALU.max).then_inc(hid_maxed, 1)

            def keep_xq(b, n):
                if is_first(b):
                    for m in range(XS):
                        dve.wait_ge(x2_stored[m], 16 * NG)
                dve.wait_ge(x_turned, b + 1)
                dve.tensor_copy(xq[:, bass.ds(b * (KD * S), KD * S)], tp_banks(n)).then_inc(xq_kept, 1)

            def round_x(b, n):
                dve.wait_ge(x_scaled, b + 1)
                wait_count(dve, x_turned, b - 1)
                dve.tensor_scalar(qi[n], x2t[n], ROUND_POS, ROUND_POS, ALU.add, ALU.subtract).then_inc(x_int, 1)

            half_way = NP2 // 2 - 1 if kept_b[NP2 // 2 - 1] else NP2 // 2

            def phase_b(t, n, g):
                if not is_first(t, 2):
                    hidden_max(t - 2, range(1))
                if not is_first(t):
                    round_x(t - 1, 1 - n)
                if not is_first(t, 2):
                    hidden_max(t - 2, range(1, half_way))
                if not is_first(t):
                    keep_xq(t - 1, 1 - n)
                if not is_first(t, 2):
                    hidden_max(t - 2, range(half_way, NP2))

            pairs(dve, phase_b)
            hidden_max(NB - 2, range(1))
            round_x(NB - 1, 1)
            hidden_max(NB - 2, range(1, half_way))
            keep_xq(NB - 1, 1)
            hidden_max(NB - 2, range(half_way, NP2))
            hidden_max(NB - 1, range(NP2))

            dve.wait_ge(hid_maxed, NB * NP2)
            link(dve.tensor_reduce(hm[:, 0, :], hmax.rearrange("p (b f) -> p f b", f=NF), AX.X, ALU.max))
            link(dve.tensor_tensor(hm[:, 1, :], hm[:, 0, :], cs1[:, :], ALU.mult))
            link(dve.tensor_tensor(hm[:, 2, :], hm[:, 1, :], bq1[:, :], ALU.add))
            link(dve.tensor_reduce(cmax[:, 2:3], hm[:, 2, :], AX.X, ALU.max))
            link(dve.tensor_scalar(cmax[:, 3:4], cmax[:, 2:3], 0.0, None, ALU.max))
            over_partitions(cmax[:, 3:4], 2)
            link(dve.tensor_scalar(s2[:, :], cmax[:, 1:2], Q_EPS, 1.0 / 255.0, ALU.max, ALU.mult))
            link(dve.reciprocal(is2[:, :], s2[:, :]))
            dve.tensor_scalar(hs[:, :], cs1[:, :], is2[:, 0:1], None, ALU.mult)
            dve.tensor_scalar(hb[:, :], bq1[:, :], is2[:, 0:1], None, ALU.mult).then_inc(h_scales, 1)
            link(dve.tensor_scalar(cs2[:, :], sw[1][:, :], s2[:, 0:1], None, ALU.mult))
            round_bias(b2c[:, :], cs2[:, :], bq2[:, :])
            for k in range(KD):
                dve.tensor_scalar(diag_cs[:, k * P:(k + 1) * P], ident[:, :], cs2[:, k:k + 1], None, ALU.mult)
                last = dve.tensor_scalar(diag_bq[:, k * P:(k + 1) * P], ident[:, :], bq2[:, k:k + 1], None, ALU.mult)
            last.then_inc(diag_ready, 1)
            dve.wait_ge(spread_ready, 3)
            dve.tensor_copy(cs2_bc[:, :], ps[:, 5, :])
            dve.tensor_copy(bq2_bc[:, :], ps[:, 6, :]).then_inc(out_scales, 1)
            dve.wait_ge(out_scales, 1)
            for n in range(2):
                dve.wait_ge(h_stored[n], 16 * NB * KEPT // 2)

            def scale_out(b):
                for i in range(NI):
                    dve.wait_ge(acc_ready, b * NI + i + 1)
                    wait_count(dve, out_ready, (b - 1) * NI + i + 1)
                    dve.tensor_tensor(ot[:, i, :], ps[:, 4 + i, :], cs2_bc[:, :], ALU.mult).then_inc(acc_read, 1)

            def add_bias(b, i):
                dve.wait_ge(x2c_loaded, (b + 1) * 16)
                dve.tensor_tensor(x2c[:, i, :], x2c[:, i, :], bq2_bc[:, :], ALU.add).then_inc(bias_added, 1)

            def add_out(b, i):
                dve.wait_ge(bias_added, b * NI + i + 1)
                dve.wait_ge(acc_read, b * NI + i + 1)
                dve.tensor_tensor(x2c[:, i, :], x2c[:, i, :], ot[:, i, :], ALU.add).then_inc(out_ready, 1)

            def phase_c(b):
                for q in range(NF):
                    if q == NI - 1 and not is_first(b):
                        scale_out(b - 1)
                    if NI <= q < 2 * NI and not is_first(b):
                        add_out(b - 1, q - NI)
                    dve.wait_ge(h_scaled, b * NF + q + 1)
                    if q < HQ - 1:
                        wait_count(dve, hq_used, (b - 1) * (NF - 1) + q + HQ + 1)
                    elif q == HQ - 1:
                        wait_count(dve, acc_ready, b * NI)
                    else:
                        dve.wait_ge(hq_used, b * (NF - 1) + q - HQ + 1)
                    dve.tensor_scalar(hq[:, q % HQ, :], hv[:, q % HV, :], ROUND_POS, ROUND_POS, ALU.add, ALU.subtract).then_inc(h_int, 1)
                for i in range(NI):
                    add_bias(b, i)

            singles(dve, phase_c, straight=2)
            scale_out(NB - 1)
            for i in range(NI):
                add_out(NB - 1, i)

        @block.tensor
        def _(pe):
            def turn_weights(w, k):
                pe.wait_ge(w_int, 4 * w + k + 1)
                if (w, k) == (0, 0):
                    pe.wait_ge(b_loaded, 32)
                    pe.transpose(ps[:, 7, 0:NF], brow[:, :], ident[0:NF, 0:NF])
                    pe.transpose(ps[:, 7, NF:NF + KD], brow2[:, :], ident[0:KD, 0:KD]).then_inc(b_turned, 1)
                    pe.wait_ge(b_kept, 1)
                for h in range(2):
                    wait_count(pe, w_kept, 8 * w + 2 * k + h - 3)
                    bank = ps[:, 4 + (2 * k + h) % 4, :].bitcast(BF16)
                    for n in range(8):
                        if w == 0:
                            at = k * 4 * D + (n % 4) * D + (2 * h + n // 4) * P
                        else:
                            at = k * F + (8 * h + n) * P
                        last = pe.transpose(bank[:, n * P:(n + 1) * P], w_int_rows[:, at:at + P], ident_b[:, :])
                    last.then_inc(w_turned, 1)

            def phase_a(j, n, g):
                pe.wait_ge(ctx_squared, j + 1)
                if is_first(j):
                    pe.wait_ge(dve_step, 1)
                for i in range(NI):
                    wait_count(pe, scan_scaled, (j - 1) * NI + i + 1)
                    for k in range(i + 1):
                        last = pe.matmul(ps[:, i, :], decay_mat[:, (i - k) * P:(i - k + 1) * P], ct[n][:, k, :],
                                         start=(k == 0), stop=(k == i))
                    last.then_inc(scan_ready, 1)
                if isinstance(j, int):
                    for w, k in weight_quarters(j - 2):
                        if w == 0:
                            turn_weights(w, k)

            batches(pe, phase_a)
            for k in range(4):
                turn_weights(1, k)

            def spread(turn):
                pe.wait_ge(diag_ready, turn)
                pe.matmul(ps[:, 4, 0:P], ones[:, :], diag[:, :], start=True, stop=True).then_inc(spread_ready, 1)

            pe.wait_ge(w_kept, 16)
            spread(1)

            def first_product(bank, b, f):
                for k in range(KD):
                    last = pe.matmul(ps[:, bank, :], w1T[:, k, f * P:(f + 1) * P], xq[:, bass.ds(b * (KD * S) + k * S, S)],
                                     start=(k == 0), stop=(k == KD - 1))
                return last

            def hidden(b, q):
                if q == 0:
                    pe.wait_ge(xq_kept, b + 1)
                if q >= 2:
                    before, bb = q - 2, b
                else:
                    before, bb = q - 2 + NP2, b - 1
                if not is_first(bb, 0):
                    if kept_b[before]:
                        pe.wait_ge(h_copied, bb * KEPT + order_b[before] - NC // 2 + 1)
                    else:
                        pe.wait_ge(hid_maxed, bb * NP2 + before + 1)
                first_product(2 * (q % 2), b, 2 * order_b[q])
                first_product(2 * (q % 2) + 1, b, 2 * order_b[q] + 1).then_inc(hid_ready, 1)

            def turn_x(b, n):
                pe.wait_ge(x_int, b + 1)
                wait_count(pe, xq_kept, b - 1)
                for k in range(KD):
                    for i in range(NI):
                        last = pe.transpose(tp_banks(n)[:, k * S + i * P:k * S + (i + 1) * P], qi[n][:, i, k * P:(k + 1) * P], ident_b[:, :])
                last.then_inc(x_turned, 1)

            def phase_b(t, n, g):
                if not is_first(t, 2):
                    for q in range(NP2 // 2):
                        hidden(t - 2, q)
                if not is_first(t):
                    turn_x(t - 1, 1 - n)
                if not is_first(t, 2):
                    for q in range(NP2 // 2, NP2):
                        hidden(t - 2, q)

            pairs(pe, phase_b, straight=2)
            for q in range(NP2 // 2):
                hidden(NB - 2, q)
            turn_x(NB - 1, 1)
            for q in range(NP2 // 2, NP2):
                hidden(NB - 2, q)
            for q in range(NP2):
                hidden(NB - 1, q)
            spread(2)

            def hidden_chunk(b, f):
                if f >= HB:
                    pe.wait_ge(h_scaled, b * NF + place_c[f - HB] + 1)
                else:
                    wait_count(pe, h_scaled, (b - 1) * NF + place_c[f - HB + NC] + 1)
                first_product(f % HB, b, f).then_inc(h_ready, 1)

            def second_product(b, q):
                pe.wait_ge(h_int, b * NF + q + 1)
                for i in range(NI):
                    if q == 0:
                        wait_count(pe, acc_read, (b - 1) * NI + i + 1)
                    last = pe.matmul(ps[:, 4 + i, :], hq[:, q % HQ, i * P:(i + 1) * P], w2T[:, order_c[q], :],
                                     start=(q == 0), stop=(q == NF - 1))
                    if q == NF - 1:
                        last.then_inc(acc_ready, 1)
                if q < NF - 1:
                    last.then_inc(hq_used, 1)

            LAG = 4
            GAP = 2

            def phase_c(b):
                per = -(-NF // NC)
                late = [(-1, q) for q in range(NF - LAG, NF)]
                own = [(0, q) for q in range(NF - LAG)]
                for f in range(NC):
                    hidden_chunk(b, f)
                    if is_first(b) and f == HB - 1:
                        pe.wait_ge(diag_ready, 3)
                        pe.matmul(ps[:, 5, :], ones[:, :], diag_cs, start=True, stop=True)
                        pe.matmul(ps[:, 6, :], ones[:, :], diag_bq, start=True, stop=True).then_inc(spread_ready, 1)
                        pe.wait_ge(out_scales, 1)
                    if late:
                        for _, q in late[:per]:
                            if not is_first(b):
                                second_product(b - 1, q)
                        late = late[per:]
                        left = GAP
                    elif left > 1:
                        left -= 1
                    else:
                        for _, q in own[:per]:
                            second_product(b, q)
                        own = own[per:]
                for _, q in own:
                    second_product(b, q)

            pe.wait_ge(hid_maxed, NB * NP2)
            singles(pe, phase_c)
            for q in range(NF - LAG, NF):
                second_product(NB - 1, q)


_INS = ["x", "ctx_1024", "L0_ffn_w1", "L0_ffn_b1", "L0_ffn_w2", "L0_ffn_b2"]


def kernel(**inputs):
    import numpy as _np
    import concourse.bacc as _bacc
    from concourse import mybir as _mybir
    from concourse.bass_utils import run_bass_kernel_spmd as _run

    nc = _bacc.Bacc("TRN2", target_bir_lowering=False, num_devices=1)
    arrays, args = {}, []
    for name in _INS:
        a = _np.ascontiguousarray(inputs[name])
        arrays[f"in_{name}_dram"] = a
        args.append(nc.dram_tensor(f"in_{name}_dram", a.shape, _mybir.dt.from_np(a.dtype), kind="ExternalInput").ap())
    shape = arrays["in_x_dram"].shape
    args.append(nc.dram_tensor("out_0_dram", shape, _mybir.dt.float32, kind="ExternalOutput").ap())
    build(nc, *args)
    r = _run(nc, [arrays], core_ids=[0])
    return r.results[0]["out_0_dram"]
```

```python
from contextlib import ExitStack

import concourse.bass as bass
from concourse import mybir

ALU = mybir.AluOpType
ACT = mybir.ActivationFunctionType
AX = mybir.AxisListType
F32 = mybir.dt.float32
BF16 = mybir.dt.bfloat16

P = 128
BANK = 512
DECAY = 0.9
LN_EPS = 1e-5
Q_EPS = 1e-8
ROUND_POS = 2.0 ** 23
ROUND_ANY = 1.5 * 2.0 ** 23
XS = 4
HQ = 8
HV = 2
HB = 4
KEPT = 4
ACT_TILES = 2
ROUND_AT, TURN_AT, KEEP_AT = 0, 4, 1
AHEAD = 2


def wait_count(eng, sem, count):
    if isinstance(count, int) and count <= 0:
        return
    eng.wait_ge(sem, count)


def build(nc, x, ctx_in, w1, b1, w2, b2, out):
    NB, S, D = x.shape
    F = w1.shape[0]
    NI = S // P
    KD = D // P
    NF = F // P
    NU = NB * NI
    ROW = NI * D
    NP2 = NF // 2
    NC = NF - 2 * KEPT

    def spread_over(n, k):
        return [(q + 1) * k // n > q * k // n for q in range(n)]

    kept_b = spread_over(NP2, KEPT)
    searched = [q for q in range(NP2) if not kept_b[q]]
    kept_at = [q for q in range(NP2) if kept_b[q]]
    order_b = [(NC // 2 + sum(kept_b[:q])) if kept_b[q] else q - sum(kept_b[:q]) for q in range(NP2)]
    kept_c = spread_over(NF, 2 * KEPT)
    order_c = [(NC + sum(kept_c[:q])) if kept_c[q] else q - sum(kept_c[:q]) for q in range(NF)]
    place_c = {f: q for q, f in enumerate(order_c)}
    assert D == BANK and S == BANK and NI == KD == 4 and NF % HQ == 0 and NB % XS == 0

    x_rows = x.rearrange("b (i p) d -> b p i d", p=P)
    ctx_rows = ctx_in.rearrange("b (i p) d -> b p i d", p=P)
    out_rows = out.rearrange("b (i p) d -> b p i d", p=P)
    w1_rows = w1.rearrange("(c p) d -> p c d", p=P)
    w2_rows = w2.rearrange("(k p) f -> p k f", p=P)
    b1_rows = b1.rearrange("(c p) -> c p", p=P)
    b2_rows = b2.rearrange("(k p) -> k p", p=P)
    h_dram = nc.dram_tensor("hidden_scratch", [NB, KEPT, P, 2 * S], F32, kind="Internal").ap()
    x2_dram = nc.dram_tensor("x2_scratch", [NB, P, ROW], F32, kind="Internal").ap()

    with ExitStack() as es:
        def sb(name, shape, dt=F32):
            return es.enter_context(nc.sbuf_tensor(name, shape, dt))

        def sem(name):
            return es.enter_context(nc.semaphore(name))

        xq = sb("xq", [P, NB * KD * S], BF16)
        arena = xq[:, :].bitcast(F32)
        o = NF * D + NF * D // 2
        rs = [arena[:, o + n * ROW:o + (n + 1) * ROW].rearrange("p (i d) -> p i d", i=NI) for n in range(2)]
        o += 2 * ROW
        ct = [arena[:, o + n * ROW:o + (n + 1) * ROW].rearrange("p (i d) -> p i d", i=NI) for n in range(XS)]
        o += XS * ROW
        xt = [arena[:, o + n * ROW:o + (n + 1) * ROW].rearrange("p (i d) -> p i d", i=NI) for n in range(XS)]
        assert o + XS * ROW == NB * KD * S // 2

        w1T = sb("w1T", [P, KD, F], BF16)
        w2T = sb("w2T", [P, NF, D], BF16)
        ident = sb("ident", [P, P])
        ident_b = sb("ident_b", [P, P], BF16)
        ones = sb("ones", [P, P])
        diag = sb("diag", [P, P])
        st1 = sb("st1", [P, XS, NI, 6])
        st2 = sb("st2", [P, XS, NI, 6])
        rowmax = sb("rowmax", [P, XS, NI])
        pw1 = sb("pw1", [P, 8, NI])
        pw2 = sb("pw2", [P, 10, NI])
        half = sb("half", [P, NI])
        neg_half = sb("neg_half", [P, NI])
        per_row = sb("per_row", [P, NI])
        eps = sb("eps", [P, NI])
        mean1 = sb("mean1", [P, XS, NI])
        rstd1 = sb("rstd1", [P, XS, NI])
        mean2 = sb("mean2", [P, NU])
        rstd2 = sb("rstd2", [P, NU])
        zrow = sb("zrow", [P, NU])
        qa = zrow
        qb = sb("qb", [P, NU])
        minus_round = sb("minus_round", [P, 1])
        wmax = [sb("wmax1", [P, NF]), sb("wmax2", [P, KD])]
        sw = [sb("sw1", [P, NF]), sb("sw2", [P, KD])]
        isw = [sb("isw1", [P, NF]), sb("isw2", [P, KD])]
        brow = sb("brow", [NF, P])
        brow2 = sb("brow2", [KD, P])
        b1c = sb("b1c", [P, NF])
        b2c = sb("b2c", [P, KD])
        rb = sb("rb", [P, 10, NF])
        s1 = sb("s1", [P, 1])
        is1 = sb("is1", [P, 1])
        s2 = sb("s2", [P, 1])
        is2 = sb("is2", [P, 1])
        cmax = sb("cmax", [P, 6])
        cs1 = sb("cs1", [P, NF])
        bq1 = sb("bq1", [P, NF])
        hm = sb("hm", [P, 3, NF])
        hs = sb("hs", [P, NF])
        hb = sb("hb", [P, NF])
        cs2 = sb("cs2", [P, KD])
        bq2 = sb("bq2", [P, KD])
        cs2_bc = sb("cs2_bc", [P, D])
        bq2_bc = sb("bq2_bc", [P, D])
        work = sb("work", [P, 4 * ROW + 2 * D])
        x2t = [work[:, n * ROW:(n + 1) * ROW].rearrange("p (i d) -> p i d", i=NI) for n in range(2)]
        qi = [work[:, (4 + n) * ROW // 2:(5 + n) * ROW // 2].bitcast(BF16).rearrange("p (i d) -> p i d", i=NI) for n in range(2)]
        hkeep = [work[:, 3 * ROW + n * 2 * S:3 * ROW + (n + 1) * 2 * S].rearrange("p (n t) -> p n t", n=2) for n in range(2)]
        hmax = work[:, 4 * ROW:4 * ROW + NB * NF]
        x2c = work[:, 0:ROW].rearrange("p (i d) -> p i d", i=NI)
        hload = [work[:, ROW + n * 2 * S:ROW + (n + 1) * 2 * S].rearrange("p (n t) -> p n t", n=2) for n in range(2)]
        ot = work[:, 2 * ROW:3 * ROW].rearrange("p (i d) -> p i d", i=NI)
        hq = work[:, 3 * ROW:3 * ROW + HQ * S // 2].bitcast(BF16).rearrange("p (n t) -> p n t", n=HQ)
        hv = work[:, 4 * ROW:4 * ROW + HV * S].rearrange("p (n t) -> p n t", n=HV)
        decay_mat = work[:, 4 * ROW:4 * ROW + S]
        diag_cs, diag_bq = ot[:, 0, :], ot[:, 1, :]
        unused = work[:, 4 * ROW + S:4 * ROW + S + D]
        w_stage = [arena[:, 0:NF * D], work[:, 0:4 * ROW]]
        w_int_rows = arena[:, NF * D:NF * D + NF * D // 2].bitcast(BF16)
        decays, impulse = xt[XS - 1][:, 0, :], xt[XS - 1][:, 1, :]

        ps = es.enter_context(nc.psum_tensor("ps", [P, 8, BANK], F32))

        consts_ready = sem("consts_ready")
        gp_step = sem("gp_step")
        ln1_step = sem("ln1_step")
        ln2_step = sem("ln2_step")
        dve_step = sem("dve_step")
        act_step = sem("act_step")
        x_loaded = [sem(f"x_loaded{n}") for n in range(XS)]
        ctx_loaded = [sem(f"ctx_loaded{n}") for n in range(XS)]
        ctx_squared = sem("ctx_squared")
        scan_ready = sem("scan_ready")
        scan_scaled = sem("scan_scaled")
        stats1_in = sem("stats1_in")
        stats1_ready = sem("stats1_ready")
        prod_done = sem("prod_done")
        x2_done = sem("x2_done")
        stats2_in = sem("stats2_in")
        stats2_used = sem("stats2_used")
        stats2_ready = sem("stats2_ready")
        x2_stored = [sem(f"x2_stored{n}") for n in range(XS)]
        w_loaded = [[sem(f"w_loaded{w}{h}") for h in range(2)] for w in range(2)]
        b_loaded = sem("b_loaded")
        w_scale = sem("w_scale")
        w_rounded = sem("w_rounded")
        w_int = sem("w_int")
        w_turned = sem("w_turned")
        w_kept = sem("w_kept")
        b_turned = sem("b_turned")
        b_kept = sem("b_kept")
        diag_ready = sem("diag_ready")
        spread_ready = sem("spread_ready")
        q_scales = sem("q_scales")
        x2_loaded = [sem(f"x2_loaded{n}") for n in range(2)]
        x_scaled = sem("x_scaled")
        x_int = sem("x_int")
        x_turned = sem("x_turned")
        xq_kept = sem("xq_kept")
        hid_ready = sem("hid_ready")
        sums_maxed = sem("sums_maxed")
        kept_maxed = sem("kept_maxed")
        h_scales = sem("h_scales")
        h_ready = sem("h_ready")
        h_scaled = sem("h_scaled")
        h_int = sem("h_int")
        acc_ready = sem("acc_ready")
        acc_read = sem("acc_read")
        out_scales = sem("out_scales")
        hq_used = sem("hq_used")
        h_copied = sem("h_copied")
        h_stored = [sem(f"h_stored{n}") for n in range(2)]
        h_loaded = [sem(f"h_loaded{n}") for n in range(2)]
        x2c_loaded = sem("x2c_loaded")
        bias_added = sem("bias_added")
        out_ready = sem("out_ready")
        out_stored = sem("out_stored")

        NG = NB // XS
        STRAIGHT = AHEAD * XS
        block = es.enter_context(nc.Block())

        def batches(eng, step, peeled=0):
            for j in range(STRAIGHT):
                step(j, j % XS, j // XS)
            with eng.Fori(AHEAD, NG - peeled) as g:
                for n in range(XS):
                    step(g * XS + n, n, g)
            for j in range(NB - peeled * XS, NB):
                step(j, j % XS, j // XS)

        def pairs(eng, step, straight=1):
            for t in range(2 * straight):
                step(t, t % 2, t // 2)
            with eng.Fori(straight, NB // 2) as g:
                for n in range(2):
                    step(g * 2 + n, n, g)

        def singles(eng, step, straight=1):
            for b in range(straight):
                step(b)
            with eng.Fori(straight, NB) as b:
                step(b)

        def is_first(j, n=1):
            return isinstance(j, int) and j < n

        def load_ctx(eng, j, n):
            eng.dma_start(ct[n], ctx_rows[bass.ds(j, 1)].rearrange("b p i d -> (b p) i d")).then_inc(ctx_loaded[n], 16)

        def weight_halves(j):
            at = {1: (0, 0), 2: (0, 1), 5: (1, 0), 6: (1, 1)}.get(j) if isinstance(j, int) else None
            return [at] if at else []

        def weight_quarters(j):
            return [(w, 2 * h + n) for w, h in weight_halves(j - 1) for n in range(2)] if isinstance(j, int) else []

        def tp_banks(n):
            return ps[:, 4 + 2 * n:6 + 2 * n, :].rearrange("p n e -> p (n e)").bitcast(BF16)

        @block.sync
        def _(sp):
            def store_x2(j, n):
                sp.wait_ge(x2_done, (j + 1) * NI)
                sp.dma_start(x2_dram[bass.ds(j, 1)].rearrange("b p m -> (b p) m"),
                             xt[n].rearrange("p i d -> p (i d)")).then_inc(x2_stored[n], 16)

            def load_x2(t, n):
                sp.dma_start(x2t[n].rearrange("p i d -> p (i d)"),
                             x2_dram[bass.ds(t, 1)].rearrange("b p m -> (b p) m")).then_inc(x2_loaded[n], 16)

            def phase_a(j, n, g):
                if is_first(j):
                    load_ctx(sp, 0, 0)
                if isinstance(j, int) and j == XS - 1:
                    sp.wait_ge(dve_step, 1)
                if not is_first(j, XS):
                    sp.wait_ge(x2_stored[n], g * 16)
                sp.dma_start(xt[n], x_rows[bass.ds(j, 1)].rearrange("b p i d -> (b p) i d")).then_inc(x_loaded[n], 16)
                for w, h in weight_halves(j):
                    rows = (NF, KD)[w]
                    part = slice(h * rows // 2, (h + 1) * rows // 2)
                    sp.dma_start(w_stage[w].rearrange("p (c d) -> p c d", c=rows)[:, part, :],
                                 (w1_rows, w2_rows)[w][:, part, :]).then_inc(w_loaded[w][h], 16)
                if isinstance(j, int) and j == 2:
                    sp.dma_start(brow[:, :], b1_rows).then_inc(b_loaded, 16)
                    sp.dma_start(brow2[:, :], b2_rows).then_inc(b_loaded, 16)
                if not is_first(j, 2):
                    store_x2(j - 2, (n - 2) % XS)

            batches(sp, phase_a)
            store_x2(NB - 2, XS - 2)
            store_x2(NB - 1, XS - 1)
            sp.wait_ge(w_int, 8)
            for t in range(2):
                load_x2(t, t)
            for n in range(XS):
                sp.wait_ge(x2_stored[n], 16 * NG)

            def store_kept(b, k):
                sp.wait_ge(h_copied, b * KEPT + k + 1)
                sp.dma_start(h_dram[bass.ds(b, 1), k].rearrange("b p m -> (b p) m"),
                             hkeep[k % 2].rearrange("p n t -> p (n t)")).then_inc(h_stored[k % 2], 16)

            def phase_b(t, n, g):
                if not is_first(t, 2):
                    sp.wait_ge(x_int, t - 1)
                    load_x2(t, n)
                if not is_first(t, 3):
                    for k in range(KEPT):
                        store_kept(t - 3, k)

            pairs(sp, phase_b, straight=2)
            for b in range(NB - 3, NB):
                for k in range(KEPT):
                    store_kept(b, k)
            for n in range(2):
                sp.wait_ge(h_stored[n], 16 * NB * KEPT // 2)

            def load_kept(b, k):
                if k >= 2:
                    sp.wait_ge(h_scaled, b * NF + place_c[NC + 2 * (k - 2) + 1] + 1)
                else:
                    wait_count(sp, h_scaled, (b - 1) * NF + place_c[NC + 2 * (k - 2 + KEPT) + 1] + 1)
                sp.dma_start(hload[k % 2].rearrange("p n t -> p (n t)"),
                             h_dram[bass.ds(b, 1), k].rearrange("b p m -> (b p) m")).then_inc(h_loaded[k % 2], 16)

            def store_out(b):
                sp.wait_ge(out_ready, (b + 1) * NI)
                sp.dma_start(out_rows[bass.ds(b, 1)].rearrange("b p i d -> (b p) i d"), x2c).then_inc(out_stored, 16)

            def phase_c(b):
                for k in range(KEPT - 1):
                    load_kept(b, k)
                if not is_first(b):
                    store_out(b - 1)
                load_kept(b, KEPT - 1)
                wait_count(sp, out_stored, b * 16)
                sp.dma_start(x2c.rearrange("p i d -> p (i d)"),
                             x2_dram[bass.ds(b, 1)].rearrange("b p m -> (b p) m")).then_inc(x2c_loaded, 16)

            singles(sp, phase_c)
            for i in range(NI):
                sp.wait_ge(out_ready, (NB - 1) * NI + i + 1)
                sp.dma_start(out_rows[NB - 1, :, i, :], x2c[:, i, :]).then_inc(out_stored, 16)
            sp.wait_ge(out_stored, 16 * (NB - 1 + NI))

        @block.gpsimd
        def _(gp):
            gp.memset(minus_round[:, :], -ROUND_ANY)
            gp.memset(half[:, :], 0.5)
            gp.memset(per_row[:, :], 1.0 / D)
            gp.memset(eps[:, :], LN_EPS)
            gp.memset(ones[:, :], 1.0)
            gp.memset(decays, DECAY)
            gp.memset(neg_half[:, :], -0.5)
            gp.memset(impulse, 0.0)
            for n in range(XS):
                gp.memset(st1[:, n, NI - ACT_TILES:NI, 5:6], 0.0)
            gp.memset(ident[:, :], 0.0)
            gp.memset(ident_b[:, :], 0.0).then_inc(gp_step, 1)
            gp.wait_ge(gp_step, 1)
            for m, w in ((impulse, S), (ident[:, :], P), (ident_b[:, :], P)):
                last = gp.affine_select(out=m, in_=m, compare_op=ALU.not_equal, fill=1.0, base=0,
                                        pattern=[[-1, w]], channel_multiplier=1)
            last.then_inc(consts_ready, 1)

            def row_stats(pw, st, mean, done, base):
                n = st.shape[1]
                me, mo, ve, vo = (st[:, :, k] for k in (1, 4, 2, 5))
                t = [pw[:, k, :] for k in range(8)]
                gp.tensor_tensor(t[0], me, mo, ALU.add)
                gp.tensor_tensor(t[1], ve, vo, ALU.add)
                gp.tensor_tensor(t[2], me, mo, ALU.subtract).then_inc(done, 1)
                gp.wait_ge(done, base + 1)
                gp.tensor_tensor(mean, t[0], half[:, 0:n], ALU.mult)
                gp.tensor_tensor(t[3], t[1], per_row[:, 0:n], ALU.mult)
                gp.tensor_tensor(t[4], t[2], half[:, 0:n], ALU.mult).then_inc(done, 1)
                gp.wait_ge(done, base + 2)
                gp.tensor_tensor(t[5], t[3], eps[:, 0:n], ALU.add)
                gp.tensor_tensor(t[6], t[4], t[4], ALU.mult).then_inc(done, 1)
                gp.wait_ge(done, base + 3)
                gp.tensor_tensor(t[7], t[5], t[6], ALU.add).then_inc(done, 1)
                return t[7]

            def second_stats(j, n):
                cols = bass.ds(j * NI, NI)
                wait_count(gp, stats2_ready, j)
                gp.wait_ge(stats2_in, j + 1)
                mean = pw2[:, 8, :]
                var = row_stats(pw2, st2[:, n], mean, ln2_step, j * 4)
                gp.wait_ge(ln2_step, j * 4 + 4)
                gp.tensor_tensor(pw2[:, 9, :], var, var, ALU.add)
                gp.tensor_tensor(zrow[:, cols], rowmax[:, n, :], mean, ALU.subtract).then_inc(stats2_used, 1)
                gp.tensor_tensor(mean2[:, cols], pw2[:, 0, :], half[:, :], ALU.mult)
                gp.tensor_tensor(rstd2[:, cols], var, neg_half[:, :], ALU.pow).then_inc(stats2_ready, 1)

            def round_weights(w, k):
                gp.wait_ge(w_scale, 2 * w + k // 2 + 1)
                rows = (NF, KD)[w] // 4
                quarter = w_stage[w][:, k * 4 * D:(k + 1) * 4 * D]
                for c in range(rows):
                    row = quarter.rearrange("p (c d) -> p c d", c=rows)[:, c, :]
                    last = gp.tensor_scalar(row, row, isw[w][:, k * rows + c:k * rows + c + 1], ROUND_ANY, ALU.mult, ALU.add)
                last.then_inc(w_rounded, 1)

            def phase_a(j, n, g):
                wait_count(gp, stats1_ready, j)
                gp.wait_ge(stats1_in, j + 1)
                gp.wait_ge(act_step, (j + 1) * (2 * ACT_TILES))
                var = row_stats(pw1, st1[:, n], mean1[:, n, :], ln1_step, j * 4)
                gp.wait_ge(ln1_step, j * 4 + 4)
                gp.tensor_tensor(rstd1[:, n, :], var, neg_half[:, 0:NI], ALU.pow).then_inc(stats1_ready, 1)
                if not is_first(j, 2):
                    second_stats(j - 2, (n - 2) % XS)
                for w, k in weight_quarters(j):
                    round_weights(w, k)

            batches(gp, phase_a)
            second_stats(NB - 2, XS - 2)
            second_stats(NB - 1, XS - 1)

        @block.scalar
        def _(act):
            def tile_stats(j, n, g):
                for m, i in enumerate(range(NI - ACT_TILES, NI)):
                    at = j * (2 * ACT_TILES) + 2 * m
                    if m == 0:
                        act.wait_ge(x_loaded[n], (g + 1) * 16)
                    wait_count(act, act_step, at)
                    mean = st1[:, n, i, 1:2]
                    act.activation(unused, xt[n][:, i, :], ACT.Copy, scale=1.0 / D, accum_out=mean).then_inc(act_step, 1)
                    act.wait_ge(act_step, at + 1)
                    act.activation(st1[:, n, i, 4:5], mean, ACT.Copy)
                    last = act.activation(unused, xt[n][:, i, :], ACT.Square, bias=mean, scale=-1.0, accum_out=st1[:, n, i, 2:3])
                    last.then_inc(act_step, 1)

            def scale_scan(j, n):
                act.wait_ge(stats1_ready, j + 1)
                for i in range(NI):
                    act.wait_ge(scan_ready, j * NI + i + 1)
                    wait_count(act, x2_done, (j - 2) * NI + i + 1)
                    act.activation(rs[n % 2][:, i, :], ps[:, i, :], ACT.Copy, scale=rstd1[:, n, i:i + 1]).then_inc(scan_scaled, 1)

            def int_weights(w, k):
                act.wait_ge(w_rounded, 4 * w + k + 1)
                if w == 1:
                    act.wait_ge(w_turned, 2 * k + 2)
                span = slice(k * 4 * D, (k + 1) * 4 * D)
                act.activation(w_int_rows[:, span], w_stage[w][:, span], ACT.Identity, bias=minus_round[:, 0:1]).then_inc(w_int, 1)

            def keep_weights(w, k):
                if (w, k) == (0, 0):
                    act.wait_ge(b_turned, 1)
                    act.activation(b1c[:, :], ps[:, 7, 0:NF], ACT.Copy)
                    act.activation(b2c[:, :], ps[:, 7, NF:NF + KD], ACT.Copy).then_inc(b_kept, 1)
                for h in range(2):
                    act.wait_ge(w_turned, 8 * w + 2 * k + h + 1)
                    bank = ps[:, 4 + (2 * k + h) % 4, :].bitcast(BF16)
                    if w == 0:
                        act.activation(w1T[:, 2 * h:2 * h + 2, k * 4 * P:(k + 1) * 4 * P], bank.rearrange("p (a f) -> p a f", a=2),
                                       ACT.Copy).then_inc(w_kept, 1)
                    else:
                        act.activation(w2T[:, 8 * h:8 * h + 8, k * P:(k + 1) * P], bank.rearrange("p (a f) -> p a f", a=8),
                                       ACT.Copy).then_inc(w_kept, 1)

            def phase_a(j, n, g):
                if is_first(j):
                    load_ctx(act, 1, 1)
                act.wait_ge(ctx_loaded[n], (g + 1) * 16)
                act.activation(ct[n], ct[n], ACT.Square).then_inc(ctx_squared, 1)
                if is_first(j):
                    for m in range(2, XS):
                        load_ctx(act, m, m)
                if not is_first(j):
                    scale_scan(j - 1, (n - 1) % XS)
                tile_stats(j, n, g)
                if not is_first(j) and not (isinstance(j, int) and j - 1 + XS >= NB):
                    load_ctx(act, j - 1 + XS, (n - 1) % XS)
                if isinstance(j, int):
                    for w, k in weight_quarters(j - 1):
                        int_weights(w, k)
                    for w, k in weight_quarters(j - 3):
                        if w == 0:
                            keep_weights(w, k)

            batches(act, phase_a, peeled=1)
            scale_scan(NB - 1, XS - 1)
            for k in range(2, 4):
                int_weights(1, k)
            for k in range(4):
                keep_weights(1, k)

            def keep_sums(b, places):
                for q in places:
                    if kept_b[q]:
                        k = order_b[q] - NC // 2
                        act.wait_ge(hid_ready, b * NP2 + q + 1)
                        if k >= 2 or not is_first(b):
                            act.wait_ge(kept_maxed, b * KEPT + k - 1)
                            act.wait_ge(h_stored[k % 2], b * (8 * KEPT) + 16 * (k // 2))
                        act.activation(hkeep[k % 2], ps[:, 2 * (q % 2):2 * (q % 2) + 2, :], ACT.Copy).then_inc(h_copied, 1)

            def phase_b(t, n, g):
                for i in range(NI):
                    if not is_first(t, 2):
                        keep_sums(t - 2, range(i * NP2 // NI, (i + 1) * NP2 // NI))
                    if i == 0:
                        act.wait_ge(x2_loaded[n], (g + 1) * 16)
                    if i == 0 and is_first(t):
                        act.wait_ge(q_scales, 1)
                    u = t * NI + i
                    last = act.activation(x2t[n][:, i, :], x2t[n][:, i, :], ACT.Relu, bias=qb[:, bass.ds(u, 1)], scale=qa[:, bass.ds(u, 1)])
                last.then_inc(x_scaled, 1)

            pairs(act, phase_b, straight=2)
            keep_sums(NB - 2, range(NP2))
            keep_sums(NB - 1, range(NP2))
            act.wait_ge(h_scales, 1)

            def phase_c(b):
                for q, f in enumerate(order_c):
                    wait_count(act, h_int, b * NF + q - HV + 1)
                    if kept_c[q]:
                        k, half_of = divmod(f - NC, 2)
                        act.wait_ge(h_loaded[k % 2], b * (8 * KEPT) + 16 * (k // 2 + 1))
                        src = hload[k % 2][:, half_of, :]
                    else:
                        act.wait_ge(h_ready, b * NC + f + 1)
                        src = ps[:, f % HB, :]
                    act.activation(hv[:, q % HV, :], src, ACT.Relu, bias=hb[:, f:f + 1], scale=hs[:, f:f + 1]).then_inc(h_scaled, 1)

            singles(act, phase_c)

        @block.vector
        def _(dve):
            chained = [0]

            def link(ins):
                chained[0] += 1
                ins.then_inc(dve_step, 1)
                dve.wait_ge(dve_step, chained[0])

            dve.wait_ge(consts_ready, 1)
            link(dve.tensor_tensor_scan(decay_mat, decays, impulse, 0.0, ALU.mult, ALU.add))

            def weight_scales(w, h):
                rows = (NF, KD)[w]
                part = slice(h * rows // 2, (h + 1) * rows // 2)
                dve.wait_ge(w_loaded[w][h], 16)
                link(dve.tensor_reduce(wmax[w][:, part], w_stage[w].rearrange("p (c d) -> p c d", c=rows)[:, part, :], AX.X,
                                       ALU.max, apply_absolute_value=True))
                link(dve.tensor_scalar(sw[w][:, part], wmax[w][:, part], Q_EPS, 1.0 / 127.0, ALU.max, ALU.mult))
                dve.reciprocal(isw[w][:, part], sw[w][:, part]).then_inc(w_scale, 1)

            def make_x2(j, n):
                dve.wait_ge(stats1_ready, j + 1)

                def product(i):
                    dve.wait_ge(scan_scaled, j * NI + i + 1)
                    dve.scalar_tensor_tensor(rs[n % 2][:, i, :], xt[n][:, i, :], mean1[:, n, i:i + 1], rs[n % 2][:, i, :],
                                             ALU.subtract, ALU.mult).then_inc(prod_done, 1)

                def stats(i):
                    dve.wait_ge(x2_done, j * NI + i + 1)
                    return dve.bn_stats(st2[:, n, i, :], xt[n][:, i, :])

                def add(i):
                    dve.tensor_tensor_reduce(xt[n][:, i, :], rs[n % 2][:, i, :], xt[n][:, i, :], 1.0, -3.0e38, ALU.add, ALU.max,
                                             rowmax[:, n, i:i + 1]).then_inc(x2_done, 1)

                product(0)
                product(1)
                wait_count(dve, stats2_used, j - XS + 1)
                dve.wait_ge(prod_done, j * NI + 1)
                product(2)
                add(0)
                dve.wait_ge(prod_done, j * NI + 2)
                product(3)
                add(1)
                dve.wait_ge(prod_done, j * NI + 3)
                stats(0)
                add(2)
                dve.wait_ge(prod_done, j * NI + 4)
                stats(1)
                add(3)
                stats(2)
                stats(3).then_inc(stats2_in, 1)

            def phase_a(j, n, g):
                dve.wait_ge(x_loaded[n], (g + 1) * 16)
                for i in range(NI - ACT_TILES):
                    last = dve.bn_stats(st1[:, n, i, :], xt[n][:, i, :])
                last.then_inc(stats1_in, 1)
                if not is_first(j):
                    make_x2(j - 1, (n - 1) % XS)
                for w, h in weight_halves(j):
                    weight_scales(w, h)

            batches(dve, phase_a)
            make_x2(NB - 1, XS - 1)

            def over_partitions(col, spread):
                dve.tensor_scalar(diag[:, :], ident[:, :], col, None, ALU.mult).then_inc(diag_ready, 1)
                dve.wait_ge(spread_ready, spread)
                link(dve.tensor_reduce(cmax[:, 1:2], ps[:, 4, 0:P], AX.X, ALU.max))

            def round_bias(b, cs, bq):
                w = b.shape[1]
                t = [rb[:, k, 0:w] for k in range(10)]
                link(dve.reciprocal(t[0], cs))
                link(dve.tensor_tensor(t[1], b, t[0], ALU.mult))
                link(dve.tensor_scalar(t[2], t[1], -ROUND_POS, ROUND_POS, ALU.max, ALU.min))
                link(dve.tensor_scalar(t[3], t[2], 0.0, ROUND_POS, ALU.max, ALU.add))
                link(dve.tensor_scalar(t[4], t[3], ROUND_POS, None, ALU.subtract))
                link(dve.tensor_scalar(t[5], t[2], 0.0, ROUND_POS, ALU.min, ALU.subtract))
                link(dve.tensor_scalar(t[6], t[5], ROUND_POS, None, ALU.add))
                link(dve.tensor_tensor(t[7], t[1], t[2], ALU.subtract))
                link(dve.tensor_tensor(t[8], t[4], t[6], ALU.add))
                link(dve.tensor_tensor(t[9], t[8], t[7], ALU.add))
                link(dve.tensor_tensor(bq, t[9], cs, ALU.mult))

            dve.wait_ge(stats2_ready, NB)
            link(dve.tensor_tensor(zrow[:, :], zrow[:, :], rstd2[:, :], ALU.mult))
            link(dve.tensor_reduce(cmax[:, 0:1], zrow[:, :], AX.X, ALU.max))
            over_partitions(cmax[:, 0:1], 1)
            link(dve.tensor_scalar(s1[:, :], cmax[:, 1:2], Q_EPS, 1.0 / 255.0, ALU.max, ALU.mult))
            link(dve.reciprocal(is1[:, :], s1[:, :]))
            link(dve.tensor_scalar(qa[:, :], rstd2[:, :], is1[:, 0:1], None, ALU.mult))
            dve.scalar_tensor_tensor(qb[:, :], mean2[:, :], -1.0, qa[:, :], ALU.mult, ALU.mult).then_inc(q_scales, 1)
            link(dve.tensor_scalar(cs1[:, :], sw[0][:, :], s1[:, 0:1], None, ALU.mult))
            dve.wait_ge(b_kept, 1)
            round_bias(b1c[:, :], cs1[:, :], bq1[:, :])

            def max_sums(b, c):
                q = searched[c]
                dve.wait_ge(hid_ready, b * NP2 + q + 1)
                dve.tensor_reduce(hmax[:, bass.ds(b * NF + 2 * order_b[q], 2)], ps[:, 2 * (q % 2):2 * (q % 2) + 2, :],
                                  AX.X, ALU.max).then_inc(sums_maxed, 1)

            def max_kept(b, c):
                for k, q in enumerate(kept_at):
                    if sum(s < q for s in searched) == c:
                        dve.wait_ge(h_copied, b * KEPT + k + 1)
                        dve.tensor_reduce(hmax[:, bass.ds(b * NF + 2 * order_b[q], 2)], hkeep[k % 2], AX.X, ALU.max).then_inc(kept_maxed, 1)

            def keep_xq(b, n):
                if is_first(b):
                    for m in range(XS):
                        dve.wait_ge(x2_stored[m], 16 * NG)
                dve.wait_ge(x_turned, b + 1)
                dve.tensor_copy(xq[:, bass.ds(b * (KD * S), KD * S)], tp_banks(n)).then_inc(xq_kept, 1)

            def round_x(b, n):
                dve.wait_ge(x_scaled, b + 1)
                wait_count(dve, x_turned, b - 1)
                dve.tensor_scalar(qi[n], x2t[n], ROUND_POS, ROUND_POS, ALU.add, ALU.subtract).then_inc(x_int, 1)

            def phase_b(t, n, g):
                for c in range(len(searched)):
                    if not is_first(t, 2):
                        max_sums(t - 2, c)
                    if c == 0 and not is_first(t, 3):
                        max_kept(t - 3, len(searched))
                    if c == ROUND_AT and not is_first(t):
                        round_x(t - 1, 1 - n)
                    if not is_first(t, 2):
                        max_kept(t - 2, c)
                    if c == KEEP_AT and not is_first(t):
                        keep_xq(t - 1, 1 - n)

            pairs(dve, phase_b, straight=2)
            phase_b(NB, 0, NB // 2)
            for c in range(len(searched)):
                max_sums(NB - 1, c)
                if c == 0:
                    max_kept(NB - 2, len(searched))
                max_kept(NB - 1, c)
            max_kept(NB - 1, len(searched))

            dve.wait_ge(sums_maxed, NB * (NP2 - KEPT))
            dve.wait_ge(kept_maxed, NB * KEPT)
            link(dve.tensor_reduce(hm[:, 0, :], hmax.rearrange("p (b f) -> p f b", f=NF), AX.X, ALU.max))
            link(dve.tensor_tensor(hm[:, 1, :], hm[:, 0, :], cs1[:, :], ALU.mult))
            link(dve.tensor_tensor(hm[:, 2, :], hm[:, 1, :], bq1[:, :], ALU.add))
            link(dve.tensor_reduce(cmax[:, 2:3], hm[:, 2, :], AX.X, ALU.max))
            link(dve.tensor_scalar(cmax[:, 3:4], cmax[:, 2:3], 0.0, None, ALU.max))
            over_partitions(cmax[:, 3:4], 2)
            link(dve.tensor_scalar(s2[:, :], cmax[:, 1:2], Q_EPS, 1.0 / 255.0, ALU.max, ALU.mult))
            link(dve.reciprocal(is2[:, :], s2[:, :]))
            dve.tensor_scalar(hs[:, :], cs1[:, :], is2[:, 0:1], None, ALU.mult)
            dve.tensor_scalar(hb[:, :], bq1[:, :], is2[:, 0:1], None, ALU.mult).then_inc(h_scales, 1)

            def output_scales():
                link(dve.tensor_scalar(cs2[:, :], sw[1][:, :], s2[:, 0:1], None, ALU.mult))
                round_bias(b2c[:, :], cs2[:, :], bq2[:, :])
                for k in range(KD):
                    dve.tensor_scalar(diag_cs[:, k * P:(k + 1) * P], ident[:, :], cs2[:, k:k + 1], None, ALU.mult)
                    last = dve.tensor_scalar(diag_bq[:, k * P:(k + 1) * P], ident[:, :], bq2[:, k:k + 1], None, ALU.mult)
                last.then_inc(diag_ready, 1)

            def keep_output_scales():
                dve.wait_ge(spread_ready, 3)
                dve.tensor_copy(cs2_bc[:, :], ps[:, 5, :])
                dve.tensor_copy(bq2_bc[:, :], ps[:, 6, :]).then_inc(out_scales, 1)

            def scale_out(b, tiles=range(NI)):
                for i in tiles:
                    dve.wait_ge(acc_ready, b * NI + i + 1)
                    wait_count(dve, out_ready, (b - 1) * NI + i + 1)
                    dve.tensor_tensor(ot[:, i, :], ps[:, 4 + i, :], cs2_bc[:, :], ALU.mult).then_inc(acc_read, 1)

            def add_bias(b, i):
                if is_first(b) and i == 0:
                    dve.wait_ge(out_scales, 1)
                dve.wait_ge(x2c_loaded, (b + 1) * 16)
                dve.tensor_tensor(x2c[:, i, :], x2c[:, i, :], bq2_bc[:, :], ALU.add).then_inc(bias_added, 1)

            def add_out(b, i):
                dve.wait_ge(bias_added, b * NI + i + 1)
                dve.wait_ge(acc_read, b * NI + i + 1)
                dve.tensor_tensor(x2c[:, i, :], x2c[:, i, :], ot[:, i, :], ALU.add).then_inc(out_ready, 1)

            def phase_c(b):
                for q in range(NF):
                    if is_first(b) and q % (HQ // 2) == 0 and q < HQ:
                        dve.wait_ge(h_stored[q // (HQ // 2)], 16 * NB * KEPT // 2)
                    if is_first(b) and q == 1:
                        output_scales()
                    if is_first(b) and q == HQ - 2:
                        keep_output_scales()
                    if q == NI - 1 and not is_first(b):
                        scale_out(b - 1)
                    if NI <= q < 2 * NI and not is_first(b):
                        add_out(b - 1, q - NI)
                    dve.wait_ge(h_scaled, b * NF + q + 1)
                    if q < HQ - 1:
                        wait_count(dve, hq_used, (b - 1) * (NF - 1) + q + HQ + 1)
                    elif q == HQ - 1:
                        wait_count(dve, acc_ready, b * NI)
                    else:
                        dve.wait_ge(hq_used, b * (NF - 1) + q - HQ + 1)
                    dve.tensor_scalar(hq[:, q % HQ, :], hv[:, q % HV, :], ROUND_POS, ROUND_POS, ALU.add, ALU.subtract).then_inc(h_int, 1)
                for i in range(NI):
                    add_bias(b, i)

            singles(dve, phase_c, straight=2)
            for i in range(NI):
                scale_out(NB - 1, (i,))
                add_out(NB - 1, i)

        @block.tensor
        def _(pe):
            def turn_weights(w, k):
                pe.wait_ge(w_int, 4 * w + k + 1)
                if (w, k) == (0, 0):
                    pe.wait_ge(b_loaded, 32)
                    pe.transpose(ps[:, 7, 0:NF], brow[:, :], ident[0:NF, 0:NF])
                    pe.transpose(ps[:, 7, NF:NF + KD], brow2[:, :], ident[0:KD, 0:KD]).then_inc(b_turned, 1)
                    pe.wait_ge(b_kept, 1)
                for h in range(2):
                    wait_count(pe, w_kept, 8 * w + 2 * k + h - 3)
                    bank = ps[:, 4 + (2 * k + h) % 4, :].bitcast(BF16)
                    for n in range(8):
                        if w == 0:
                            at = k * 4 * D + (n % 4) * D + (2 * h + n // 4) * P
                        else:
                            at = k * F + (8 * h + n) * P
                        last = pe.transpose(bank[:, n * P:(n + 1) * P], w_int_rows[:, at:at + P], ident_b[:, :])
                    last.then_inc(w_turned, 1)

            def phase_a(j, n, g):
                pe.wait_ge(ctx_squared, j + 1)
                if is_first(j):
                    pe.wait_ge(dve_step, 1)
                for i in range(NI):
                    wait_count(pe, scan_scaled, (j - 1) * NI + i + 1)
                    for k in range(i + 1):
                        last = pe.matmul(ps[:, i, :], decay_mat[:, (i - k) * P:(i - k + 1) * P], ct[n][:, k, :],
                                         start=(k == 0), stop=(k == i))
                    last.then_inc(scan_ready, 1)
                if isinstance(j, int):
                    for w, k in weight_quarters(j - 2):
                        if w == 0:
                            turn_weights(w, k)

            batches(pe, phase_a)
            for k in range(4):
                turn_weights(1, k)

            def spread(turn):
                pe.wait_ge(diag_ready, turn)
                pe.matmul(ps[:, 4, 0:P], ones[:, :], diag[:, :], start=True, stop=True).then_inc(spread_ready, 1)

            pe.wait_ge(w_kept, 16)
            spread(1)

            def first_product(bank, b, f):
                for k in range(KD):
                    last = pe.matmul(ps[:, bank, :], w1T[:, k, f * P:(f + 1) * P], xq[:, bass.ds(b * (KD * S) + k * S, S)],
                                     start=(k == 0), stop=(k == KD - 1))
                return last

            def hidden(b, q):
                if q == 0:
                    pe.wait_ge(xq_kept, b + 1)
                if q >= 2:
                    before, bb = q - 2, b
                else:
                    before, bb = q - 2 + NP2, b - 1
                if not is_first(bb, 0):
                    if kept_b[before]:
                        pe.wait_ge(h_copied, bb * KEPT + order_b[before] - NC // 2 + 1)
                    else:
                        pe.wait_ge(sums_maxed, bb * (NP2 - KEPT) + searched.index(before) + 1)
                first_product(2 * (q % 2), b, 2 * order_b[q])
                first_product(2 * (q % 2) + 1, b, 2 * order_b[q] + 1).then_inc(hid_ready, 1)

            def turn_x(b, n):
                pe.wait_ge(x_int, b + 1)
                wait_count(pe, xq_kept, b - 1)
                for k in range(KD):
                    for i in range(NI):
                        last = pe.transpose(tp_banks(n)[:, k * S + i * P:k * S + (i + 1) * P], qi[n][:, i, k * P:(k + 1) * P], ident_b[:, :])
                last.then_inc(x_turned, 1)

            def phase_b(t, n, g):
                if not is_first(t, 2):
                    for q in range(TURN_AT):
                        hidden(t - 2, q)
                if not is_first(t):
                    turn_x(t - 1, 1 - n)
                if not is_first(t, 2):
                    for q in range(TURN_AT, NP2):
                        hidden(t - 2, q)

            pairs(pe, phase_b, straight=2)
            phase_b(NB, 0, NB // 2)
            for q in range(NP2):
                hidden(NB - 1, q)
            spread(2)

            def hidden_chunk(b, f):
                if f >= HB:
                    pe.wait_ge(h_scaled, b * NF + place_c[f - HB] + 1)
                else:
                    wait_count(pe, h_scaled, (b - 1) * NF + place_c[f - HB + NC] + 1)
                first_product(f % HB, b, f).then_inc(h_ready, 1)

            def second_product(b, q):
                pe.wait_ge(h_int, b * NF + q + 1)
                for i in range(NI):
                    if q == 0:
                        wait_count(pe, acc_read, (b - 1) * NI + i + 1)
                    last = pe.matmul(ps[:, 4 + i, :], hq[:, q % HQ, i * P:(i + 1) * P], w2T[:, order_c[q], :],
                                     start=(q == 0), stop=(q == NF - 1))
                    if q == NF - 1:
                        last.then_inc(acc_ready, 1)
                if q < NF - 1:
                    last.then_inc(hq_used, 1)

            LAG = 4
            GAP = 2

            def phase_c(b):
                per = -(-NF // NC)
                late = list(range(NF - LAG, NF))
                own = list(range(NF - LAG))
                if is_first(b):
                    for f in range(NC):
                        hidden_chunk(b, f)
                        if f == NC - 3:
                            pe.wait_ge(diag_ready, 3)
                            pe.matmul(ps[:, 5, :], ones[:, :], diag_cs, start=True, stop=True)
                            pe.matmul(ps[:, 6, :], ones[:, :], diag_bq, start=True, stop=True).then_inc(spread_ready, 1)
                    pe.wait_ge(out_scales, 1)
                    for q in own:
                        second_product(b, q)
                    return
                for f in range(NC):
                    hidden_chunk(b, f)
                    if late:
                        for q in late[:per]:
                            second_product(b - 1, q)
                        late = late[per:]
                        left = GAP
                    elif left > 1:
                        left -= 1
                    else:
                        for q in own[:per]:
                            second_product(b, q)
                        own = own[per:]
                for q in own:
                    second_product(b, q)

            pe.wait_ge(sums_maxed, NB * len(searched))
            singles(pe, phase_c)
            for q in range(NF - LAG, NF):
                second_product(NB - 1, q)


_INS = ["x", "ctx_1024", "L0_ffn_w1", "L0_ffn_b1", "L0_ffn_w2", "L0_ffn_b2"]


def kernel(**inputs):
    import numpy as _np
    import concourse.bacc as _bacc
    from concourse import mybir as _mybir
    from concourse.bass_utils import run_bass_kernel_spmd as _run

    nc = _bacc.Bacc("TRN2", target_bir_lowering=False, num_devices=1)
    arrays, args = {}, []
    for name in _INS:
        a = _np.ascontiguousarray(inputs[name])
        arrays[f"in_{name}_dram"] = a
        args.append(nc.dram_tensor(f"in_{name}_dram", a.shape, _mybir.dt.from_np(a.dtype), kind="ExternalInput").ap())
    shape = arrays["in_x_dram"].shape
    args.append(nc.dram_tensor("out_0_dram", shape, _mybir.dt.float32, kind="ExternalOutput").ap())
    build(nc, *args)
    r = _run(nc, [arrays], core_ids=[0])
    return r.results[0]["out_0_dram"]
```
